# Optimizing a Trainium2 kernel written in Bass

```python
import numpy as np
import jax
import jax.numpy as jnp

def _softmax(x, axis=-1):
    return jax.nn.softmax(x, axis=axis)

def _gelu(x):
    return jax.nn.gelu(x, approximate=True)

def _silu(x):
    return jax.nn.silu(x)

def _sigmoid(x):
    return jax.nn.sigmoid(x)

def _layernorm(x, axis=-1, eps=1e-05):
    m = jnp.mean(x, axis=axis, keepdims=True)
    v = jnp.var(x, axis=axis, keepdims=True)
    return (x - m) / jnp.sqrt(v + eps)

def _scatter_add(tgt, idx, src, axis=0):
    return tgt.at[idx].add(src)

def _segment_sum(src, seg, n):
    return jax.ops.segment_sum(src, seg, n)
kernel_name = 'mk_adaln_ffn_d1_seqx_r8_f6dec9'

def setup_inputs(seed: int=0):
    np.random.seed(seed)
    _w = jnp.asarray

    def _rec_inputs():
        import jax
        import jax.numpy as jnp
        _rk = jax.random.key(seed)
        x = -8.015e-05 + 0.9999 * jax.random.normal(jax.random.fold_in(_rk, 1), (128, 32, 256), jnp.float32)
        _lenS = 32 - jax.random.randint(jax.random.fold_in(_rk, 7), (128,), 0, max(1, 32 // 4) + 1, jnp.int32)
        _lenS2 = 32 - jax.random.randint(jax.random.fold_in(_rk, 8), (128,), 0, max(1, 32 // 4) + 1, jnp.int32)
        cond_1024 = 0.00191187 + 0.999416 * jax.random.normal(jax.random.fold_in(_rk, 11), (128, 128), jnp.float32)
        return (x, cond_1024)
    x, cond_1024 = _rec_inputs()

    def _L0_cond_setup():
        import jax, jax.numpy as jnp
        import numpy as np
        B, N, V_DIM, Q_DIM = (32, 100, 256, 128)
        key = jax.random.key(seed)
        k1, k2, k3, k4 = jax.random.split(key, 4)
        v = jax.random.normal(k1, (B, N, V_DIM), dtype=jnp.float32)
        q = jax.random.normal(k2, (B, Q_DIM), dtype=jnp.float32)
        W3 = jax.random.normal(k3, (Q_DIM, V_DIM), dtype=jnp.float32) * (1.0 / np.sqrt(Q_DIM))
        b3 = jnp.zeros((V_DIM,), dtype=jnp.float32)
        W2 = jax.random.normal(k4, (V_DIM, V_DIM), dtype=jnp.float32) * (1.0 / np.sqrt(V_DIM))
        b2 = jnp.zeros((V_DIM,), dtype=jnp.float32)
        return {'v': v, 'q': q, 'W3': W3, 'b3': b3, 'W2': W2, 'b2': b2}
    _L0_cond_all = _L0_cond_setup()
    _L0_cond_in = {k: v for k, v in _L0_cond_all.items() if k in ('W3', 'b3', 'W2', 'b2')}
    del _L0_cond_all

    def _L0_ffn_setup():
        import jax, jax.numpy as jnp
        import numpy as np
        B, S, H, I, E, F, K, R, TOPK = (1, 128, 256, 176, 64, 8, 8, 8, 6)
        ISH = 2 * I

        def _fused_linear(x, W, qa, qb, scale, w):
            out = x @ W.T
            a = jnp.einsum('th,krh->tkr', x, qa)
            b = jnp.einsum('tkr,khr->tkh', a, qb)
            mix = jnp.einsum('tkh,tk->th', b, w)
            return out + scale[None, :] * mix

        def _moe_forward(hidden_states, gate_weight, inv_mapping, mask_up_W, gate_W, gate_qa, gate_qb, gate_scale, up_W, up_qa, up_qb, up_scale, down_W, down_qa, down_qb, down_scale, sh_gate_W, sh_up_W, sh_down_W):
            b, s, h = hidden_states.shape
            x = hidden_states.reshape(-1, h)
            T = x.shape[0]
            scores = jax.nn.softmax(x @ gate_weight.T, axis=-1)
            topk_w, topk_idx = jax.lax.top_k(scores, TOPK)
            w_dense = jnp.zeros((T, E), x.dtype).at[jnp.arange(T)[:, None], topk_idx].add(topk_w)
            flat = w_dense[:, inv_mapping]
            scalar = flat.sum(-1)
            soft = jax.nn.softmax(jnp.where(flat == 0, -1000000000.0, flat), axis=-1)

            def expert(muW, gW, gqa, gqb, gs, uW, uqa, uqb, us, dW, dqa, dqb, ds, w):
                xe = x + w @ muW.T
                gate = jax.nn.silu(_fused_linear(xe, gW, gqa, gqb, gs, w))
                up = _fused_linear(xe, uW, uqa, uqb, us, w)
                return _fused_linear(gate * up, dW, dqa, dqb, ds, w)
            outs = jax.vmap(expert, in_axes=(0,) * 13 + (1,))(mask_up_W, gate_W, gate_qa, gate_qb, gate_scale, up_W, up_qa, up_qb, up_scale, down_W, down_qa, down_qb, down_scale, soft)
            y = jnp.einsum('fth,tf->th', outs, scalar).reshape(b, s, h)
            sh = jax.nn.silu(hidden_states @ sh_gate_W.T) * (hidden_states @ sh_up_W.T) @ sh_down_W.T
            return y + sh
        key = jax.random.key(seed)
        ks = jax.random.split(key, 20)
        g = lambda k, shape, s=0.02: jax.random.normal(k, shape, jnp.float32) * s
        return {'hidden_states': jax.random.normal(ks[0], (B, S, H), jnp.float32), 'gate_weight': g(ks[1], (E, H)), 'inv_mapping': jnp.arange(E, dtype=jnp.int32).reshape(F, K), 'mask_up_W': g(ks[2], (F, H, K)), 'gate_W': g(ks[3], (F, I, H)), 'gate_qa': g(ks[4], (F, K, R, H)), 'gate_qb': g(ks[5], (F, K, I, R)), 'gate_scale': jnp.full((F, I), 0.1, jnp.float32), 'up_W': g(ks[6], (F, I, H)), 'up_qa': g(ks[7], (F, K, R, H)), 'up_qb': g(ks[8], (F, K, I, R)), 'up_scale': jnp.full((F, I), 0.1, jnp.float32), 'down_W': g(ks[9], (F, H, I)), 'down_qa': g(ks[10], (F, K, R, I)), 'down_qb': g(ks[11], (F, K, H, R)), 'down_scale': jnp.full((F, H), 0.1, jnp.float32), 'sh_gate_W': g(ks[12], (ISH, H)), 'sh_up_W': g(ks[13], (ISH, H)), 'sh_down_W': g(ks[14], (H, ISH))}
    _L0_ffn_all = _L0_ffn_setup()
    _L0_ffn_in = {k: v for k, v in _L0_ffn_all.items() if k in ('gate_weight', 'inv_mapping', 'mask_up_W', 'gate_W', 'gate_qa', 'gate_qb', 'gate_scale', 'up_W', 'up_qa', 'up_qb', 'up_scale', 'down_W', 'down_qa', 'down_qb', 'down_scale', 'sh_gate_W', 'sh_up_W', 'sh_down_W')}
    del _L0_ffn_all
    return {'x': x, 'cond_1024': cond_1024, 'L0_cond_W3': _L0_cond_in['W3'], 'L0_cond_b3': _L0_cond_in['b3'], 'L0_cond_W2': _L0_cond_in['W2'], 'L0_cond_b2': _L0_cond_in['b2'], 'L0_ffn_gate_weight': _L0_ffn_in['gate_weight'], 'L0_ffn_inv_mapping': _L0_ffn_in['inv_mapping'], 'L0_ffn_mask_up_W': _L0_ffn_in['mask_up_W'], 'L0_ffn_gate_W': _L0_ffn_in['gate_W'], 'L0_ffn_gate_qa': _L0_ffn_in['gate_qa'], 'L0_ffn_gate_qb': _L0_ffn_in['gate_qb'], 'L0_ffn_gate_scale': _L0_ffn_in['gate_scale'], 'L0_ffn_up_W': _L0_ffn_in['up_W'], 'L0_ffn_up_qa': _L0_ffn_in['up_qa'], 'L0_ffn_up_qb': _L0_ffn_in['up_qb'], 'L0_ffn_up_scale': _L0_ffn_in['up_scale'], 'L0_ffn_down_W': _L0_ffn_in['down_W'], 'L0_ffn_down_qa': _L0_ffn_in['down_qa'], 'L0_ffn_down_qb': _L0_ffn_in['down_qb'], 'L0_ffn_down_scale': _L0_ffn_in['down_scale'], 'L0_ffn_sh_gate_W': _L0_ffn_in['sh_gate_W'], 'L0_ffn_sh_up_W': _L0_ffn_in['sh_up_W'], 'L0_ffn_sh_down_W': _L0_ffn_in['sh_down_W']}

def reference(x, cond_1024, L0_cond_W3, L0_cond_b3, L0_cond_W2, L0_cond_b2, L0_ffn_gate_weight, L0_ffn_inv_mapping, L0_ffn_mask_up_W, L0_ffn_gate_W, L0_ffn_gate_qa, L0_ffn_gate_qb, L0_ffn_gate_scale, L0_ffn_up_W, L0_ffn_up_qa, L0_ffn_up_qb, L0_ffn_up_scale, L0_ffn_down_W, L0_ffn_down_qa, L0_ffn_down_qb, L0_ffn_down_scale, L0_ffn_sh_gate_W, L0_ffn_sh_up_W, L0_ffn_sh_down_W):
    import jax
    import jax.numpy as jnp

    def _L0_cond_ref(v, q, W3, b3, W2, b2):
        import jax, jax.numpy as jnp
        import numpy as np
        B, N, V_DIM, Q_DIM = (32, 100, 256, 128)
        q_emb = jax.nn.relu(q @ W3 + b3)
        n = v.shape[1]
        v_sum = jnp.sum(v, axis=1, keepdims=True)
        x = (n * v + v_sum) * q_emb[:, None, :]
        return jax.nn.relu(x @ W2 + b2)

    def _L0_ffn_ref(hidden_states, gate_weight, inv_mapping, mask_up_W, gate_W, gate_qa, gate_qb, gate_scale, up_W, up_qa, up_qb, up_scale, down_W, down_qa, down_qb, down_scale, sh_gate_W, sh_up_W, sh_down_W):
        import jax, jax.numpy as jnp
        import numpy as np
        B, S, H, I, E, F, K, R, TOPK = (1, 128, 256, 176, 64, 8, 8, 8, 6)
        ISH = 2 * I

        def _fused_linear(x, W, qa, qb, scale, w):
            out = x @ W.T
            a = jnp.einsum('th,krh->tkr', x, qa)
            b = jnp.einsum('tkr,khr->tkh', a, qb)
            mix = jnp.einsum('tkh,tk->th', b, w)
            return out + scale[None, :] * mix

        def _moe_forward(hidden_states, gate_weight, inv_mapping, mask_up_W, gate_W, gate_qa, gate_qb, gate_scale, up_W, up_qa, up_qb, up_scale, down_W, down_qa, down_qb, down_scale, sh_gate_W, sh_up_W, sh_down_W):
            b, s, h = hidden_states.shape
            x = hidden_states.reshape(-1, h)
            T = x.shape[0]
            scores = jax.nn.softmax(x @ gate_weight.T, axis=-1)
            topk_w, topk_idx = jax.lax.top_k(scores, TOPK)
            w_dense = jnp.zeros((T, E), x.dtype).at[jnp.arange(T)[:, None], topk_idx].add(topk_w)
            flat = w_dense[:, inv_mapping]
            scalar = flat.sum(-1)
            soft = jax.nn.softmax(jnp.where(flat == 0, -1000000000.0, flat), axis=-1)

            def expert(muW, gW, gqa, gqb, gs, uW, uqa, uqb, us, dW, dqa, dqb, ds, w):
                xe = x + w @ muW.T
                gate = jax.nn.silu(_fused_linear(xe, gW, gqa, gqb, gs, w))
                up = _fused_linear(xe, uW, uqa, uqb, us, w)
                return _fused_linear(gate * up, dW, dqa, dqb, ds, w)
            outs = jax.vmap(expert, in_axes=(0,) * 13 + (1,))(mask_up_W, gate_W, gate_qa, gate_qb, gate_scale, up_W, up_qa, up_qb, up_scale, down_W, down_qa, down_qb, down_scale, soft)
            y = jnp.einsum('fth,tf->th', outs, scalar).reshape(b, s, h)
            sh = jax.nn.silu(hidden_states @ sh_gate_W.T) * (hidden_states @ sh_up_W.T) @ sh_down_W.T
            return y + sh
        return _moe_forward(hidden_states, gate_weight, inv_mapping, mask_up_W, gate_W, gate_qa, gate_qb, gate_scale, up_W, up_qa, up_qb, up_scale, down_W, down_qa, down_qb, down_scale, sh_gate_W, sh_up_W, sh_down_W)
    x = x + _L0_ffn_ref(_L0_cond_ref(x, cond_1024, L0_cond_W3, L0_cond_b3, L0_cond_W2, L0_cond_b2), L0_ffn_gate_weight, L0_ffn_inv_mapping, L0_ffn_mask_up_W, L0_ffn_gate_W, L0_ffn_gate_qa, L0_ffn_gate_qb, L0_ffn_gate_scale, L0_ffn_up_W, L0_ffn_up_qa, L0_ffn_up_qb, L0_ffn_up_scale, L0_ffn_down_W, L0_ffn_down_qa, L0_ffn_down_qb, L0_ffn_down_scale, L0_ffn_sh_gate_W, L0_ffn_sh_up_W, L0_ffn_sh_down_W)
    return x

_drawn_inputs = setup_inputs


def setup_inputs(seed=0):
    import zlib

    import numpy as np

    out = dict(_drawn_inputs(seed))
    spreads = {'L0_cond_b3': (0.0, 0.1),
     'L0_cond_b2': (0.0, 0.8),
     'L0_ffn_gate_scale': (0.10000000149011612, 0.6),
     'L0_ffn_up_scale': (0.10000000149011612, 0.6),
     'L0_ffn_down_scale': (0.10000000149011612, 0.6)}
    factors = {'L0_ffn_mask_up_W': 64.0,
     'L0_ffn_gate_qa': 8.0,
     'L0_ffn_gate_qb': 8.0,
     'L0_ffn_up_qa': 8.0,
     'L0_ffn_up_qb': 8.0,
     'L0_ffn_down_qa': 8.0,
     'L0_ffn_down_qb': 8.0}
    for name, (base, spread) in spreads.items():
        noise = np.random.default_rng([zlib.crc32(name.encode()), seed]).standard_normal(out[name].shape)
        drawn = base * np.exp(spread * noise) if base else spread * noise
        out[name] = jnp.asarray(drawn.astype(out[name].dtype))
    for name, factor in factors.items():
        out[name] = (out[name] * factor).astype(out[name].dtype)
    return out
```

```python
from contextlib import ExitStack, nullcontext

import concourse.bass as bass
from concourse import mybir

F32 = mybir.dt.float32
F32R = mybir.dt.float32r
I32 = mybir.dt.int32
ALU = mybir.AluOpType
ACT = mybir.ActivationFunctionType
AX = mybir.AxisListType.X

P = 128
BATCH, SEQ, H, COND = 128, 32, 256, 128
TOKENS = BATCH * SEQ
CH = 512
NCH = TOKENS // CH
CB = CH // SEQ
TT = CH // P
KH = H // P
E, F, K, R, TOPK = 64, 8, 8, 8, 6
KR = K * R
I = 176
TAIL = I - P
CW = KR + TAIL
ISH = 2 * I
SB = [(0, P), (P, P), (2 * P, ISH - 2 * P)]

XA, XGA, XC, XUB, XW = 0, P, 2 * P, 2 * P + CW, 3 * P + CW
QB = KH * XW
QGA, QGC, QUC, QUB = QB, QB + P, QB + P + CW, QB + P + 2 * CW
QW = 2 * P + 2 * CW
DN = QB + QW
SPLIT = DN + 2 * H
PIECES = 6
PW = -(-SPLIT // (2 * PIECES)) * 2
SPLITW = PW * PIECES
ADR = SPLITW
MU = ADR + 2 * KR
RAWW = MU + KH * P
BW2, BGW, BSG, BSD = 0, KH * H, KH * H + KH * E, KH * H + KH * E + KH * 2 * ISH
BOOT = BSD + 3 * H
CONSTS = P + 3
NEG = -1.0e9
GONE = -3.0e38
ABSENT = 3.0e38


class Unit:

    def __init__(self, e, c, k, p, w):
        self.e, self.c, self.k, self.p, self.w = e, c, k, p, w
        self.now, self.last, self.same = k + 1, k + p, k


def steps(eng):
    def unit(i, t, j=0):
        return Unit(i * 2 + t // NCH, j * 2 + t % NCH, i * NCH + (j + t // 2), t % 2, (t // NCH) % 2)

    yield None, unit(0, 0), unit(0, 1), (0, None), None
    pairs = F // 2
    with eng.Fori(0, pairs) as i:
        for t0 in (0, NCH):
            with eng.Fori(0, (NCH - 2) // 2) as j:
                for t in (t0 + 1, t0 + 2):
                    yield unit(i, t - 1, j), unit(i, t, j), unit(i, t + 1, j), (t, j), i < pairs - 1
            for t in (t0 + NCH - 1, t0 + NCH):
                yield unit(i, t - 1), unit(i, t), unit(i, t + 1), (t, None), i < pairs - 1


def build(nc, xT, condT, W3, vecs, consts, inv, boot, raw_d, scale_d, outT):
    soft_d = nc.dram_tensor("soft_scratch", (NCH * (E + F), CH), F32, kind="Internal").ap()
    packed_d = nc.dram_tensor("packed_scratch", (NCH * 3 * E, CH), F32, kind="Internal").ap()

    with ExitStack() as ctx:
        def sb(name, cols, dt=F32):
            return ctx.enter_context(nc.sbuf_tensor(name, [P, cols], dt))

        def carve(arena, sizes):
            out, at = [], 0
            for n in sizes:
                out.append(arena[:, at:at + n])
                at += n
            assert at <= arena.shape[1], (at, arena.shape)
            return out

        y = sb("y", KH * TOKENS)[:, :].rearrange("p (k t) -> p k t", k=KH)
        hs = sb("h_split", 2 * KH * TOKENS, F32R)[:, :].rearrange("p (s k t) -> p s k t", s=2, k=KH)
        W_even = sb("W_even", 2 * SPLITW, F32R)
        ADt = sb("down_adapter", 2 * 2 * P, F32R)[:, :].rearrange("p (w k m) -> p w k m", w=2, k=2)
        A3 = sb("a_packed", 2 * P, F32R)[:, :].rearrange("p (w m) -> p w m", w=2)
        Gh = sb("G_hi", XW, F32R)
        raw = sb("raw", RAWW)
        scb = sb("scales", QW + H)
        q = sb("q_emb", KH * BATCH)[:, :].rearrange("p (k b) -> p k b", k=KH)
        cst = sb("consts", CONSTS)
        eye, lomask, rowno = cst[:, 0:P], cst[:, P:P + 1], cst[:, P + 1:P + 3]
        onehot = sb("onehot", 2 * E)
        vec = sb("vectors", 2 * KH)
        b3s, b2s = vec[:, 0:KH], vec[:, KH:2 * KH]

        RA = sb("arena_r", 16 * CH + 2 * SPLITW, F32R)
        FA = sb("arena_f", 13 * CH)

        (W2s, GWs, SGs, SDs, xcs, hSs, sfs) = carve(
            RA, [2 * KH * H, KH * 2 * E, 2 * KH * 2 * ISH, 2 * 3 * H, 2 * KH * CH, 3 * 2 * CH, 2 * CH])
        W2s = W2s.rearrange("p (s k m) -> p s k m", s=2, k=KH)
        GWs = GWs.rearrange("p (k m) -> p k m", k=KH)
        SGs = SGs.rearrange("p (s k m) -> p s k m", s=2, k=KH)
        SDs = SDs.rearrange("p (s b m) -> p s b m", s=2, b=3)
        xcs = xcs.rearrange("p (s k t) -> p s k t", s=2, k=KH)
        hSs = hSs.rearrange("p (b s t) -> p b s t", b=3, s=2)
        sfs = sfs.rearrange("p (s t) -> p s t", s=2)
        (xc_, hf_, RLs, lg, ex, rep, wsel, z, st, wTs, sTs, sS, mS, top, sm, rs, gm, gs, vs) = carve(
            FA, [KH * CH, KH * CH, CH, TT * E, TT * E, TT * E, TT * E, TT * E, TT * (E + F), TT * E, CH, CH, CH,
                 TT * 8, TT, TT, TT * F, TT * F, KH * CB])
        xc = xc_.rearrange("p (k t) -> p k t", k=KH)
        hf = hf_.rearrange("p (k t) -> p k t", k=KH)
        lg, ex, rep, wsel, z, st, top = (v.rearrange("p (j e) -> p j e", j=TT)
                                         for v in (lg, ex, rep, wsel, z, st, top))
        W3s, cTs, invs = xc_[:, 0:H], xc_[:, H:H + BATCH], z[:, 0, :].bitcast(I32)
        invf, invn = ex[:, 0, :], ex[:, 1, :]
        SDraw = hf_[:, 0:3 * H]

        r2 = carve(RA, [CH] * 16 + [2 * SPLITW])
        Vg, Vu, Xg, Xu, Ahi, Alo, Rhi, Rlo = (r2[2 * n:2 * n + 2] for n in range(8))
        Wt = [W_even[:, :].rearrange("p (s m) -> p s m", s=2), r2[16].rearrange("p (s m) -> p s m", s=2)]
        f2 = carve(FA, [CH] * 13)
        wexp, wdn, scl = (f2[2 * n:2 * n + 2] for n in range(3))
        ap, sA, sC, mA, mC, adc, adp = f2[6:13]

        PS = ctx.enter_context(nc.psum_tensor("ps", [P, 8, CH], F32))
        pA, pB, pC, pa, pad, pG = (PS[:, n, :] for n in range(6))
        pY = PS[:, 6:8, :]
        TAILS = slice(KR, CW)

        def sem(name):
            return ctx.enter_context(nc.semaphore(name))

        def sems(names):
            return [sem(n) for n in names.split()]

        def pairs(names):
            return [[sem(n + "_even"), sem(n + "_odd")] for n in names.split()]

        (consts_in, x_in, boot_in, sd_in, raw_in, soft_out, y_out) = sems(
            "consts_in x_in boot_in sd_in raw_in soft_out y_out")
        (inv_f, inv_n, inv_w, inv_c, onehot_ok, q_mm, q_ok, boot_hi, w2_lo, boot_lo) = sems(
            "inv_f inv_n inv_w inv_c onehot_ok q_mm q_ok boot_hi w2_lo boot_lo")
        (vsum_ok, xsum_ok, xc_ok, xc_hi, xc_lo, h_mm, hf_ok, h_hi, h_lo, rl_mm, rl_cp, tl_mm, lg_ok) = sems(
            "vsum_ok xsum_ok xc_ok xc_hi xc_lo h_mm hf_ok h_hi h_lo rl_mm rl_cp tl_mm lg_ok")
        (top_ok, absent_ok, rep_ok, dl_ok, ex_ok, sm_ok, rs_ok, wsel_ok, wn_ok, wT_mm, wT_cp, fl_mm) = sems(
            "top_ok absent_ok rep_ok dl_ok ex_ok sm_ok rs_ok wsel_ok wn_ok wT_mm wT_cp fl_mm")
        (z_neg, z_all, tot_ok, gm_ok, z_sub, z_exp, gs_ok, gr_ok, soft_ok, sT_mm, sT_cp, s_hi, s_lo) = sems(
            "z_neg z_all tot_ok gm_ok z_sub z_exp gs_ok gr_ok soft_ok sT_mm sT_cp s_hi s_lo")
        (sg_mm, s_sil, s_mul, s_ahi, s_alo, sy_mm, sy_add) = sems("sg_mm s_sil s_mul s_ahi s_alo sy_mm sy_add")
        a_mm, gA_mm, gB_mm, gC_mm, ad_mm, y_mm = pairs("a_mm gA_mm gB_mm gC_mm ad_mm y_mm")
        ap_ok, vg_lo, vu_lo, ad_sum, adp_ok, ad_lo, mulA, loA, mulC, loC, y_add = pairs(
            "ap_ok vg_lo vu_lo ad_sum adp_ok ad_lo mulA loA mulC loC y_add")
        vg_hi, vu_hi, xg_hi, xu_hi, ad_cp, silA, ad_hi, hiA, silC, hiC = pairs(
            "vg_hi vu_hi xg_hi xu_hi ad_cp silA ad_hi hiA silC hiC")
        scA, scC, wexp_in, wdn_in, scl_in, pk_in = pairs("scA scC wexp_in wdn_in scl_in pk_in")
        (foldQ, foldR, piece_hi, piece_lo, adw_hi, adw_lo, g_mm, g_hi, a3_ok, g3g_ok, g3u_ok, zeros_ok) = sems(
            "foldQ foldR piece_hi piece_lo adw_hi adw_lo g_mm g_hi a3_ok g3g_ok g3u_ok zeros_ok")

        def f32(v):
            return v.bitcast(F32)

        def when(eng, t, steps_, cond):
            return eng.If(cond) if t in steps_ else nullcontext()

        def real(e):
            if isinstance(e, int):
                return e
            return nc.s_assert_within(e, 0, F - 1, skip_runtime_bounds_check_because="left out in the last pair")

        def chunk(c):
            if isinstance(c, int):
                return c
            return nc.s_assert_within(c, 0, NCH - 1, skip_runtime_bounds_check_because="left out after the last chunk")

        block = ctx.enter_context(nc.Block())

        @block.sync
        def _(sp):
            sp.dma_start(y[:, :, 0:CH], xT[:, :, 0:CH]).then_inc(x_in, 16)
            sp.dma_start(raw[:, 0:BSD], boot[:, 0:BSD]).then_inc(boot_in, 16)
            sp.dma_start(SDraw, boot[:, BSD:BOOT]).then_inc(sd_in, 16)
            with sp.Fori(1, NCH) as c:
                sp.wait_ge(x_in, c * 16)
                sp.dma_start(y[:, :, bass.ds(c * CH, CH)], xT[:, :, bass.ds(c * CH, CH)]).then_inc(x_in, 16)

            def load_raw(e):
                e = real(e)
                sp.dma_start(raw[:, 0:RAWW], raw_d[bass.ds(e * P, P), :]).then_inc(raw_in, 16)
                row = scale_d[bass.ds(e, 1), :]
                sp.dma_start(scb[:, :], bass.AP(row.tensor, row.offset, [[0, P], [1, QW + H]])).then_inc(raw_in, 16)

            sp.wait_ge(boot_hi, 4)
            sp.wait_ge(w2_lo, 1)
            sp.wait_ge(boot_lo, 3)
            load_raw(0)

            with sp.Fori(0, NCH) as c:
                sp.wait_ge(sT_cp, c + 1)
                sp.dma_start(soft_d[bass.ds(c * (E + F), E + F), :], sTs[0:E + F, :]).then_inc(soft_out, 16)
                sp.wait_ge(s_hi, c + 1)
                sp.dma_start(packed_d[bass.ds(c * 3 * E, E), :], f32(sfs[0:E, 0, :])).then_inc(soft_out, 16)
                sp.dma_start(packed_d[bass.ds(c * 3 * E + 2 * E, E), :], f32(sfs[0:E, 0, :])).then_inc(soft_out, 16)
                sp.wait_ge(s_lo, c + 1)
                sp.dma_start(packed_d[bass.ds(c * 3 * E + E, E), :], f32(sfs[0:E, 1, :])).then_inc(soft_out, 16)
            sp.wait_ge(soft_out, 4 * 16 * NCH)
            sp.wait_ge(sy_add, NCH)
            sp.wait_ge(zeros_ok, 3)

            def load_unit(n):
                e = real(n.e)
                row = soft_d[bass.ds(n.c * (E + F) + e * K, K), :]
                part = packed_d[bass.ds(n.c * 3 * E + e * K, K), :]
                total = soft_d[bass.ds(n.c * (E + F) + e + E, 1), :]
                packed = bass.AP(part.tensor, part.offset, [[E * CH, 3], [CH, K], [1, CH]])
                sp.wait_ge(ap_ok[n.p], n.same)
                sp.dma_start(wexp[n.p], bass.AP(row.tensor, row.offset, [[0, 2 * R], [CH, K], [1, CH]])
                             ).then_inc(wexp_in[n.p], 16)
                sp.wait_ge(a_mm[n.p], n.same)
                sp.wait_ge(gC_mm[n.p], n.same)
                sp.dma_start(f32(Xu[n.p][0:3 * K, :]), packed).then_inc(pk_in[n.p], 16)
                sp.dma_start(f32(Xg[n.p][KR:KR + 3 * K, :]), packed).then_inc(pk_in[n.p], 16)
                sp.wait_ge(scA[n.p], n.same)
                sp.wait_ge(scC[n.p], n.same)
                sp.dma_start(scl[n.p], bass.AP(total.tensor, total.offset, [[0, P], [1, CH]])
                             ).then_inc(scl_in[n.p], 16)
                sp.wait_ge(adp_ok[n.p], n.same)
                sp.dma_start(wdn[n.p][0:KR, :], bass.AP(row.tensor, row.offset, [[0, R], [CH, K], [1, CH]])
                             ).then_inc(wdn_in[n.p], 16)

            def next_raw(e):
                sp.wait_ge(piece_hi, e * PIECES)
                sp.wait_ge(piece_lo, e * PIECES)
                sp.wait_ge(adw_hi, e)
                sp.wait_ge(adw_lo, e)
                sp.wait_ge(g_mm, e)
                load_raw(e)

            for prev, cur, nxt, (t, _j), more in steps(sp):
                if prev is None:
                    load_unit(cur)
                    next_raw(1)
                    load_unit(nxt)
                    continue
                with when(sp, t, (15, 16), more):
                    load_unit(nxt)
                if t in (7, 15):
                    with sp.If(more):
                        next_raw(cur.e + 2)
            with sp.Fori(0, NCH // 2) as c:
                for p in (0, 1):
                    sp.wait_ge(y_add[p], c + ((F - 1) * NCH // 2 + 1))
                    sp.dma_start(outT[:, :, bass.ds((c * 2 + p) * CH, CH)], y[:, :, bass.ds((c * 2 + p) * CH, CH)]
                                 ).then_inc(y_out, 16)
            sp.wait_ge(y_out, 16 * NCH)

        @block.tensor
        def _(pe):
            def product(out, parts, first=True, last=True):
                for n, (lhsT, rhs) in enumerate(parts):
                    mm = pe.matmul(out, lhsT, rhs, start=first and n == 0, stop=last and n == len(parts) - 1)
                return mm

            def three(w_hi, w_lo, v_hi, v_lo):
                return [(w_hi, v_hi), (w_lo, v_hi), (w_hi, v_lo)]

            pe.wait_ge(consts_in, 16 * 5)
            for m in range(KH):
                mm = product(PS[:, 2, m * BATCH:(m + 1) * BATCH], [(W3s[:, m * P:(m + 1) * P], cTs)])
            mm.then_inc(q_mm, 1)

            def h_products(c):
                pe.wait_ge(xc_hi, c + 1)
                pe.wait_ge(xc_lo, c + 1)
                pe.wait_ge(hf_ok, c)
                for m in range(KH):
                    ms = slice(m * P, (m + 1) * P)
                    mm = product(PS[:, m, :], [x for k in range(KH) for x in
                                               three(W2s[:, 0, k, ms], W2s[:, 1, k, ms], xcs[:, 0, k, :], xcs[:, 1, k, :])])
                mm.then_inc(h_mm, 1)

            def h_of(c):
                return [[hs[:, s, k, bass.ds(c * CH, CH)] for k in range(KH)] for s in (0, 1)]

            pe.wait_ge(boot_hi, 1)
            pe.wait_ge(w2_lo, 1)
            pe.wait_ge(onehot_ok, 1)
            h_products(0)
            pe.wait_ge(boot_hi, 4)
            pe.wait_ge(boot_lo, 3)
            with pe.Fori(0, NCH) as c:
                hh, hl = h_of(c)

                def shared_up(b):
                    at, n = SB[b]
                    pe.wait_ge(s_mul, c * 3 + b)
                    for g in (0, 1):
                        ms = slice(2 * at + g * n, 2 * at + (g + 1) * n)
                        mm = product(PS[0:n, 4 + g, :], [x for k in range(KH) for x in
                                                         three(SGs[:, 0, k, ms], SGs[:, 1, k, ms], hh[k], hl[k])])
                    mm.then_inc(sg_mm, 1)

                def shared_down(b):
                    n = SB[b][1]
                    pe.wait_ge(s_ahi, c * 3 + b + 1)
                    pe.wait_ge(s_alo, c * 3 + b + 1)
                    if b == 0:
                        pe.wait_ge(sy_add, c)
                    for m in range(KH):
                        ms = slice(m * P, (m + 1) * P)
                        mm = product(PS[:, 6 + m, :], three(SDs[0:n, 0, b, ms], SDs[0:n, 1, b, ms],
                                                            hSs[0:n, b, 0, :], hSs[0:n, b, 1, :]),
                                     first=b == 0, last=b == 2)
                    mm.then_inc(sy_mm, 1)

                pe.wait_ge(h_hi, c + 1)
                pe.wait_ge(h_lo, c + 1)
                pe.wait_ge(sT_cp, c)
                product(PS[:, 2, :], [(GWs[:, k, :], v[k]) for k in range(KH) for v in (hh, hl)]).then_inc(rl_mm, 1)
                shared_up(0)
                pe.wait_ge(rl_cp, c + 1)
                pe.wait_ge(tot_ok, c)
                pe.wait_ge(z_all, c)
                for j in range(TT):
                    mm = pe.transpose(PS[:, 3, j * P:(j + 1) * P], RLs[:, j * P:(j + 1) * P], eye)
                mm.then_inc(tl_mm, 1)
                shared_up(1)
                shared_down(0)
                shared_up(2)
                pe.wait_ge(wn_ok, c + 1)
                for j in range(TT // 2):
                    mm = pe.transpose(PS[:, 2, j * P:(j + 1) * P], wsel[:, 2 * j:2 * j + 2, :], eye)
                mm.then_inc(wT_mm, 1)
                shared_down(1)
                pe.wait_ge(wT_cp, c + 1)
                pe.wait_ge(lg_ok, c + 1)
                for j in range(TT // 2):
                    mm = product(PS[:, 3, j * P:(j + 1) * P], [(wTs[:, j * P:(j + 1) * P], onehot[:, :])])
                mm.then_inc(fl_mm, 1)
                shared_down(2)
                with pe.If(c < NCH - 1):
                    h_products(c + 1)
                pe.wait_ge(soft_ok, c + 1)
                pe.wait_ge(tot_ok, c + 1)
                for j in range(TT):
                    mm = pe.transpose(PS[0:E + F, 2, j * P:(j + 1) * P], st[:, j, :], eye)
                mm.then_inc(sT_mm, 1)

            def w(n, s, at, width=P, rows=slice(0, P)):
                return Wt[n.w][rows, s, at:at + width]

            def from_h(n, at, width=P):
                hh, hl = h_of(n.c)
                return [x for k in range(KH) for x in
                        three(w(n, 0, k * XW + at, width), w(n, 1, k * XW + at, width), hh[k], hl[k])]

            def g_products(e):
                pe.wait_ge(raw_in, e * 32 + 32)
                pe.wait_ge(a3_ok, e)
                pe.wait_ge(g3g_ok, e)
                pe.wait_ge(g3u_ok, e)
                product(pG[:, 0:XW], [(raw[:, MU + k * P:MU + (k + 1) * P], raw[:, k * XW:(k + 1) * XW])
                                      for k in range(KH)]).then_inc(g_mm, 1)

            def adapters_in(n, fresh):
                if fresh:
                    pe.wait_ge(piece_hi, n.e * PIECES + PIECES)
                    pe.wait_ge(piece_lo, n.e * PIECES + PIECES)
                    pe.wait_ge(a3_ok, n.e + 1)
                pe.wait_ge(ap_ok[1 - n.p], n.last)
                product(pa, from_h(n, XA), last=False)
                pe.wait_ge(pk_in[n.p], n.same * 32 + 32)
                product(pa, [(A3[0:3 * K, n.w, :], Xu[n.p][0:3 * K, :])], first=False).then_inc(a_mm[n.p], 1)

            def down_adapter(n, fresh):
                if fresh:
                    pe.wait_ge(adw_hi, n.e + 1)
                    pe.wait_ge(adw_lo, n.e + 1)
                pe.wait_ge(hiA[n.p], n.now)
                pe.wait_ge(loA[n.p], n.now)
                pe.wait_ge(hiC[n.p], n.now)
                pe.wait_ge(loC[n.p], n.now)
                pe.wait_ge(ad_sum[1 - n.p], n.last)
                product(pad, [(ADt[:, n.w, 0, :], Ahi[n.p]), (ADt[:, n.w, 0, :], Alo[n.p]),
                              (ADt[TAILS, n.w, 1, :], Rhi[n.p][TAILS, :]),
                              (ADt[TAILS, n.w, 1, :], Rlo[n.p][TAILS, :])]).then_inc(ad_mm[n.p], 1)

            def gate_up(n, fresh):
                packed = slice(0, KR + 3 * K)
                if fresh:
                    pe.wait_ge(g3g_ok, n.e + 1)
                    pe.wait_ge(g3u_ok, n.e + 1)
                pe.wait_ge(silA[1 - n.p], n.last)
                product(pA, from_h(n, XGA), last=False)
                pe.wait_ge(vg_hi[n.p], n.now)
                pe.wait_ge(vg_lo[n.p], n.now)
                pe.wait_ge(xg_hi[n.p], n.now)
                product(pA, [(w(n, 0, QGA), Vg[n.p]), (w(n, 1, QGA, P, packed), Xg[n.p][packed, :])],
                        first=False).then_inc(gA_mm[n.p], 1)
                pe.wait_ge(vu_hi[n.p], n.now)
                pe.wait_ge(vu_lo[n.p], n.now)
                pe.wait_ge(xu_hi[n.p], n.now)
                pe.wait_ge(mulA[1 - n.p], n.last)
                product(pB, from_h(n, XUB) + [(w(n, 0, QUB), Vu[n.p]), (w(n, 1, QUB), Xu[n.p])]
                        ).then_inc(gB_mm[n.p], 1)
                pe.wait_ge(mulC[1 - n.p], n.last)
                up = slice(KR, P)
                product(pC[0:CW, :], from_h(n, XC, CW) + [
                    (w(n, 0, QGC, CW), Vg[n.p]), (w(n, 1, QGC, CW, packed), Xg[n.p][packed, :]),
                    (w(n, 0, QUC, CW), Vu[n.p]), (w(n, 1, QUC, CW, up), Xu[n.p][up, :])]).then_inc(gC_mm[n.p], 1)

            def down(n):
                pe.wait_ge(ad_hi[n.p], n.now)
                pe.wait_ge(ad_lo[n.p], n.now)
                pe.wait_ge(y_add[1 - n.p], n.last)
                r = slice(0, CW)
                for m in range(KH):
                    dA, dR = DN + m * P, DN + H + m * P
                    mm = product(pY[:, m, :], three(w(n, 0, dA), w(n, 1, dA), Ahi[n.p], Alo[n.p]) +
                                 three(w(n, 0, dR, P, r), w(n, 1, dR, P, r), Rhi[n.p][r, :], Rlo[n.p][r, :]))
                mm.then_inc(y_mm[n.p], 1)

            g_products(0)
            for prev, cur, nxt, (t, _j), more in steps(pe):
                if prev is None:
                    adapters_in(cur, True)
                    adapters_in(nxt, False)
                    gate_up(cur, True)
                    g_products(1)
                    continue
                with when(pe, t, (15, 16), more):
                    adapters_in(nxt, t in (7, 15))
                down_adapter(prev, t in (1, 9))
                with when(pe, t, (16,), more):
                    gate_up(cur, t in (8, 16))
                down(prev)
                if t in (8, 16):
                    with pe.If(more):
                        g_products(cur.e + 1)

        @block.scalar
        def _(act):
            def copy(out, in_):
                return act.activation(out, in_, ACT.Copy)

            act.dma_start(W3s, W3).then_inc(consts_in, 16)
            act.dma_start(cTs, condT).then_inc(consts_in, 16)
            act.dma_start(vec[:, :], vecs).then_inc(consts_in, 16)
            act.dma_start(cst[:, :], consts).then_inc(consts_in, 16)
            act.dma_start(invs, bass.AP(inv.tensor, 0, [[0, P], [1, E]])).then_inc(consts_in, 16)

            act.wait_ge(boot_in, 16)
            copy(W2s[:, 0].rearrange("p k m -> p (k m)"), raw[:, BW2:BGW]).then_inc(boot_hi, 1)
            copy(GWs[:, :, 0:E], raw[:, BGW:BSG].rearrange("p (k m) -> p k m", k=KH)).then_inc(boot_hi, 1)
            copy(SGs[:, 0].rearrange("p k m -> p (k m)"), raw[:, BSG:BSD]).then_inc(boot_hi, 1)

            def condition_high(c):
                act.wait_ge(xc_ok, c + 1)
                act.wait_ge(h_mm, c)
                copy(xcs[:, 0], xc).then_inc(xc_hi, 1)

            def h_high(c):
                act.wait_ge(h_mm, c + 1)
                act.wait_ge(h_hi, c)
                act.wait_ge(h_lo, c)
                for m in range(KH):
                    last = act.activation(hf[:, m, :], PS[:, m, :], ACT.Relu, bias=b2s[:, m:m + 1])
                last.then_inc(hf_ok, 1)
                act.wait_ge(hf_ok, c + 1)
                copy(hs[:, 0, :, bass.ds(chunk(c) * CH, CH)], hf).then_inc(h_hi, 1)

            condition_high(0)
            act.wait_ge(sd_in, 16)
            copy(SDs[:, 0].rearrange("p b m -> p (b m)"), SDraw).then_inc(boot_hi, 1)
            act.wait_ge(boot_hi, 4)
            act.wait_ge(boot_lo, 3)
            h_high(0)
            with act.Fori(0, NCH) as c:
                def shared_silu(b):
                    n = SB[b][1]
                    act.wait_ge(sg_mm, c * 3 + b + 1)
                    act.wait_ge(s_mul, c * 3 + b)
                    act.activation(sS[0:n, :], PS[0:n, 4, :], ACT.Silu).then_inc(s_sil, 1)

                def shared_high(b):
                    n = SB[b][1]
                    act.wait_ge(s_mul, c * 3 + b + 1)
                    act.wait_ge(sy_mm, c * 3)
                    copy(hSs[0:n, b, 0, :], mS[0:n, :]).then_inc(s_ahi, 1)

                act.wait_ge(rl_mm, c + 1)
                act.wait_ge(tl_mm, c)
                copy(RLs, PS[:, 2, :]).then_inc(rl_cp, 1)
                shared_silu(0)
                shared_high(0)
                act.wait_ge(dl_ok, c + 1)
                act.activation(ex, ex, ACT.Exp).then_inc(ex_ok, 1)
                shared_silu(1)
                shared_high(1)
                shared_silu(2)
                shared_high(2)
                act.wait_ge(wT_mm, c + 1)
                act.wait_ge(fl_mm, c)
                copy(wTs, PS[:, 2, 0:TT * E]).then_inc(wT_cp, 1)
                with act.If(c < NCH - 1):
                    condition_high(c + 1)
                act.wait_ge(z_sub, c + 1)
                act.activation(z, z, ACT.Exp).then_inc(z_exp, 1)
                with act.If(c < NCH - 1):
                    h_high(c + 1)
                act.wait_ge(sT_mm, c + 1)
                act.wait_ge(soft_out, c * 64)
                act.wait_ge(s_lo, c)
                copy(sTs[0:E + F, :], PS[0:E + F, 2, :]).then_inc(sT_cp, 1)
                act.wait_ge(sT_cp, c + 1)
                copy(sfs[0:E, 0, :], sTs[0:E, :]).then_inc(s_hi, 1)

            def g_high(e):
                act.wait_ge(g_mm, e + 1)
                act.wait_ge(a3_ok, e)
                act.wait_ge(g3g_ok, e)
                act.wait_ge(g3u_ok, e)
                copy(Gh[:, :], pG[:, 0:XW]).then_inc(g_hi, 1)

            def adapters_high(n):
                g, u = slice(0, KR), slice(KR, P)
                act.wait_ge(ap_ok[n.p], n.now)
                act.wait_ge(gC_mm[n.p], n.same)
                copy(Vg[n.p][g, :], ap[g, :]).then_inc(vg_hi[n.p], 1)
                copy(Vu[n.p][u, :], ap[u, :]).then_inc(vu_hi[n.p], 1)
                copy(Xg[n.p][g, :], ap[g, :]).then_inc(xg_hi[n.p], 1)
                copy(Xu[n.p][u, :], ap[u, :]).then_inc(xu_hi[n.p], 1)

            act.wait_ge(sy_add, NCH)
            act.wait_ge(s_lo, NCH)
            act.wait_ge(soft_out, 64 * NCH)
            g_high(0)
            for prev, cur, nxt, (t, _j), more in steps(act):
                if prev is None:
                    adapters_high(cur)
                with when(act, t, (15, 16), more):
                    adapters_high(nxt)
                if prev is not None:
                    act.wait_ge(ad_mm[prev.p], prev.now)
                    act.wait_ge(ad_sum[1 - prev.p], prev.last)
                    copy(adc[0:KR, :], pad[KR:P, :]).then_inc(ad_cp[prev.p], 1)
                with when(act, t, (16,), more):
                    act.wait_ge(gA_mm[cur.p], cur.now)
                    act.wait_ge(mulA[1 - cur.p], cur.last)
                    act.activation(sA, pA, ACT.Silu).then_inc(silA[cur.p], 1)
                if prev is not None:
                    act.wait_ge(adp_ok[prev.p], prev.now)
                    act.wait_ge(y_mm[prev.p], prev.same)
                    copy(Rhi[prev.p][0:KR, :], adp[0:KR, :]).then_inc(ad_hi[prev.p], 1)
                with when(act, t, (16,), more):
                    act.wait_ge(scA[cur.p], cur.now)
                    act.wait_ge(y_mm[cur.p], cur.same)
                    copy(Ahi[cur.p], mA).then_inc(hiA[cur.p], 1)
                    act.wait_ge(gC_mm[cur.p], cur.now)
                    act.wait_ge(mulC[1 - cur.p], cur.last)
                    act.activation(sC[TAILS, :], pC[0:TAIL, :], ACT.Silu).then_inc(silC[cur.p], 1)
                    act.wait_ge(scC[cur.p], cur.now)
                    copy(Rhi[cur.p][TAILS, :], mC[TAILS, :]).then_inc(hiC[cur.p], 1)
                if prev is None:
                    g_high(1)
                if t in (8, 16):
                    with act.If(more):
                        g_high(cur.e + 1)

        @block.vector
        def _(dve):
            sub = ALU.subtract

            dve.wait_ge(consts_in, 16 * 5)
            dve.tensor_copy(invf, invs).then_inc(inv_f, 1)
            dve.wait_ge(inv_f, 1)
            dve.tensor_scalar(invn, invf, 0.0, float(E), ALU.is_lt, ALU.mult).then_inc(inv_n, 1)
            dve.wait_ge(inv_n, 1)
            dve.tensor_tensor(invf, invf, invn, ALU.add).then_inc(inv_w, 1)
            dve.wait_ge(inv_w, 1)
            dve.tensor_scalar(invf, invf, 0.0, float(E - 1), ALU.max, ALU.min).then_inc(inv_c, 1)
            dve.wait_ge(inv_c, 1)
            for n in (0, 1):
                last = dve.tensor_scalar(onehot[:, n * E:(n + 1) * E], invf, rowno[:, n:n + 1], None, ALU.is_equal)
            last.then_inc(onehot_ok, 1)
            dve.wait_ge(q_mm, 1)
            for m in range(KH):
                last = dve.tensor_scalar(q[:, m, :], PS[:, 2, m * BATCH:(m + 1) * BATCH], b3s[:, m:m + 1], 0.0,
                                         ALU.add, ALU.max)
            last.then_inc(q_ok, 1)

            def condition(c):
                xs = y[:, :, bass.ds(chunk(c) * CH, CH)].rearrange("p k (b s) -> p k b s", s=SEQ)
                dve.wait_ge(x_in, c * 16 + 16)
                dve.wait_ge(xsum_ok, c)
                dve.tensor_reduce(vs.rearrange("p (k b) -> p k b", k=KH), xs, AX, ALU.add).then_inc(vsum_ok, 1)
                dve.wait_ge(vsum_ok, c + 1)
                dve.wait_ge(xc_hi, c)
                dve.wait_ge(xc_lo, c)
                for k in range(KH):
                    last = dve.scalar_tensor_tensor(
                        xc[:, k, :].rearrange("p (b s) -> p b s", s=SEQ), xs[:, k], float(SEQ),
                        vs[:, k * CB:(k + 1) * CB].unsqueeze(2).broadcast_to([P, CB, SEQ]), ALU.mult, ALU.add)
                last.then_inc(xsum_ok, 1)

            condition(0)
            dve.wait_ge(boot_hi, 1)
            dve.tensor_tensor(W2s[:, 1].rearrange("p k m -> p (k m)"), raw[:, BW2:BGW],
                              f32(W2s[:, 0].rearrange("p k m -> p (k m)")), sub).then_inc(w2_lo, 1)
            with dve.Fori(0, NCH) as c:
                def shared_mul(b):
                    n = SB[b][1]
                    dve.wait_ge(s_sil, c * 3 + b + 1)
                    dve.wait_ge(s_ahi, c * 3 + b)
                    dve.wait_ge(s_alo, c * 3 + b)
                    dve.tensor_tensor(mS[0:n, :], PS[0:n, 5, :], sS[0:n, :], ALU.mult).then_inc(s_mul, 1)

                def by_group(v):
                    return v.rearrange("p j (f k) -> p (j f) k", k=K)

                dve.wait_ge(tl_mm, c + 1)
                dve.wait_ge(dl_ok, c)
                dve.wait_ge(rep_ok, c)
                dve.tensor_reduce(lg, PS[:, 3, :].rearrange("p (j s e) -> p j e s", j=TT, s=2), AX, ALU.add
                                  ).then_inc(lg_ok, 1)
                dve.wait_ge(lg_ok, c + 1)
                shared_mul(0)
                for j in range(TT):
                    last = dve.max(top[:, j, :], lg[:, j, :])
                last.then_inc(top_ok, 1)
                dve.wait_ge(top_ok, c + 1)
                dve.memset(top[:, :, TOPK:8], ABSENT).then_inc(absent_ok, 1)
                dve.wait_ge(absent_ok, c + 1)
                dve.wait_ge(ex_ok, c)
                dve.wait_ge(wsel_ok, c)
                dve.tensor_tensor(ex, lg, top[:, :, 0:1].broadcast_to([P, TT, E]), sub).then_inc(dl_ok, 1)
                for j in range(TT):
                    last = dve.match_replace(rep[:, j, :], top[:, j, :], lg[:, j, :], GONE)
                last.then_inc(rep_ok, 1)
                with dve.If(c < NCH - 1):
                    condition(c + 1)
                dve.wait_ge(ex_ok, c + 1)
                dve.tensor_reduce(sm, ex, AX, ALU.add).then_inc(sm_ok, 1)
                dve.wait_ge(sm_ok, c + 1)
                dve.reciprocal(rs, sm).then_inc(rs_ok, 1)
                shared_mul(1)
                dve.wait_ge(rep_ok, c + 1)
                dve.wait_ge(wT_mm, c)
                dve.scalar_tensor_tensor(wsel, rep, GONE / 2, ex, ALU.is_le, ALU.mult).then_inc(wsel_ok, 1)
                dve.wait_ge(wsel_ok, c + 1)
                dve.wait_ge(rs_ok, c + 1)
                dve.tensor_tensor(wsel, wsel, rs.unsqueeze(2).broadcast_to([P, TT, E]), ALU.mult).then_inc(wn_ok, 1)
                shared_mul(2)
                flat = PS[:, 3, 0:TT * E].rearrange("p (j e) -> p j e", j=TT)
                dve.wait_ge(fl_mm, c + 1)
                dve.wait_ge(soft_ok, c)
                dve.tensor_scalar(z, flat, 0.0, NEG, ALU.is_equal, ALU.mult).then_inc(z_neg, 1)
                dve.wait_ge(sT_mm, c)
                dve.tensor_reduce(st[:, :, E:E + F], flat.rearrange("p j (f k) -> p j f k", k=K), AX, ALU.add
                                  ).then_inc(tot_ok, 1)
                dve.wait_ge(z_neg, c + 1)
                dve.tensor_tensor(z, z, flat, ALU.add).then_inc(z_all, 1)
                dve.wait_ge(z_all, c + 1)
                dve.tensor_reduce(gm, by_group(z), AX, ALU.max).then_inc(gm_ok, 1)
                dve.wait_ge(gm_ok, c + 1)
                dve.tensor_tensor(by_group(z), by_group(z), gm.unsqueeze(2).broadcast_to([P, TT * F, K]), sub
                                  ).then_inc(z_sub, 1)
                dve.wait_ge(z_exp, c + 1)
                dve.tensor_reduce(gs, by_group(z), AX, ALU.add).then_inc(gs_ok, 1)
                dve.wait_ge(gs_ok, c + 1)
                dve.reciprocal(gs, gs).then_inc(gr_ok, 1)
                dve.wait_ge(gr_ok, c + 1)
                dve.tensor_tensor(st[:, :, 0:E].rearrange("p j (f k) -> p j f k", k=K),
                                  z.rearrange("p j (f k) -> p j f k", k=K),
                                  gs.rearrange("p (j f) -> p j f", j=TT).unsqueeze(3).broadcast_to([P, TT, F, K]),
                                  ALU.mult).then_inc(soft_ok, 1)
                yc = y[:, :, bass.ds(c * CH, CH)]
                dve.wait_ge(sy_mm, c * 3 + 3)
                dve.tensor_tensor(yc, yc, pY, ALU.add).then_inc(sy_add, 1)

            def g_rows(rows, e, out, cols, ok):
                dve.wait_ge(g_hi, e + 1)
                dve.scalar_tensor_tensor(out[rows, :], f32(Gh[rows, cols]), lomask[rows, :], pG[rows, cols],
                                         ALU.mult, ALU.add).then_inc(ok, 1)

            low, high = slice(0, 3 * K), slice(KR, KR + 3 * K)

            def g_adapters(e, wp):
                g_rows(low, e, A3[:, wp, :], slice(XA, XA + P), a3_ok)

            def g_gate_up(e, wp):
                dve.wait_ge(piece_lo, e * PIECES + PIECES)
                g_rows(high, e, Wt[wp][:, 1, QGA:QGA + P + CW], slice(XGA, XGA + P + CW), g3g_ok)
                g_rows(low, e, Wt[wp][:, 1, QUB:QUB + P], slice(XUB, XUB + P), g3u_ok)

            def adapters_weighted(n):
                dve.wait_ge(a_mm[n.p], n.now)
                dve.wait_ge(wexp_in[n.p], n.same * 16 + 16)
                dve.wait_ge(vg_hi[1 - n.p], n.last)
                dve.wait_ge(vu_hi[1 - n.p], n.last)
                dve.wait_ge(xg_hi[1 - n.p], n.last)
                dve.wait_ge(xu_hi[1 - n.p], n.last)
                dve.wait_ge(vg_lo[1 - n.p], n.last)
                dve.wait_ge(vu_lo[1 - n.p], n.last)
                dve.tensor_tensor(ap, pa, wexp[n.p], ALU.mult).then_inc(ap_ok[n.p], 1)

            def adapters_low(n):
                g, u = slice(0, KR), slice(KR, P)
                dve.wait_ge(gC_mm[n.p], n.same)
                dve.wait_ge(vg_hi[n.p], n.now)
                dve.tensor_tensor(Vg[n.p][u, :], ap[g, :], f32(Vg[n.p][g, :]), sub).then_inc(vg_lo[n.p], 1)
                dve.wait_ge(vu_hi[n.p], n.now)
                dve.tensor_tensor(Vu[n.p][g, :], ap[u, :], f32(Vu[n.p][u, :]), sub).then_inc(vu_lo[n.p], 1)

            def add_y(n):
                yc = y[:, :, bass.ds(n.c * CH, CH)]
                dve.wait_ge(y_mm[n.p], n.now)
                dve.wait_ge(y_add[1 - n.p], n.last)
                dve.tensor_tensor(yc, yc, pY, ALU.add).then_inc(y_add[n.p], 1)

            dve.wait_ge(soft_out, 64 * NCH)
            dve.wait_ge(zeros_ok, 3)
            g_adapters(0, 0)
            g_gate_up(0, 0)
            for prev, cur, nxt, (t, _j), more in steps(dve):
                if prev is None:
                    adapters_weighted(cur)
                    adapters_low(cur)
                with when(dve, t, (15, 16), more):
                    adapters_weighted(nxt)
                    adapters_low(nxt)
                if prev is not None:
                    n = prev
                    dve.wait_ge(ad_cp[n.p], n.now)
                    dve.wait_ge(ad_hi[1 - n.p], n.last)
                    dve.wait_ge(ad_lo[1 - n.p], n.last)
                    dve.tensor_tensor(adp[0:KR, :], pad[0:KR, :], adc[0:KR, :], ALU.add).then_inc(ad_sum[n.p], 1)
                    dve.wait_ge(ad_sum[n.p], n.now)
                    dve.wait_ge(wdn_in[n.p], n.same * 16 + 16)
                    dve.tensor_tensor(adp[0:KR, :], adp[0:KR, :], wdn[n.p][0:KR, :], ALU.mult).then_inc(adp_ok[n.p], 1)
                    dve.wait_ge(ad_hi[n.p], n.now)
                    dve.tensor_tensor(Rlo[n.p][0:KR, :], adp[0:KR, :], f32(Rhi[n.p][0:KR, :]), sub
                                      ).then_inc(ad_lo[n.p], 1)
                with when(dve, t, (16,), more):
                    n = cur
                    dve.wait_ge(silA[n.p], n.now)
                    dve.wait_ge(gB_mm[n.p], n.now)
                    dve.wait_ge(hiA[1 - n.p], n.last)
                    dve.wait_ge(loA[1 - n.p], n.last)
                    dve.tensor_tensor(mA, pB, sA, ALU.mult).then_inc(mulA[n.p], 1)
                    dve.wait_ge(hiA[n.p], n.now)
                    dve.tensor_tensor(Alo[n.p], mA, f32(Ahi[n.p]), sub).then_inc(loA[n.p], 1)
                    dve.wait_ge(silC[n.p], n.now)
                    dve.wait_ge(hiC[1 - n.p], n.last)
                    dve.wait_ge(loC[1 - n.p], n.last)
                    dve.tensor_tensor(mC[TAILS, :], pC[TAILS, :], sC[TAILS, :], ALU.mult).then_inc(mulC[n.p], 1)
                if prev is not None:
                    add_y(prev)
                with when(dve, t, (16,), more):
                    n = cur
                    dve.wait_ge(hiC[n.p], n.now)
                    dve.wait_ge(y_mm[n.p], n.same)
                    dve.tensor_tensor(Rlo[n.p][TAILS, :], mC[TAILS, :], f32(Rhi[n.p][TAILS, :]), sub
                                      ).then_inc(loC[n.p], 1)
                if prev is None:
                    g_adapters(1, 1)
                if t in (8, 16):
                    with dve.If(more):
                        g_adapters(cur.e + 1, 1 - cur.w)
                if t == 7:
                    g_gate_up(cur.e + 1, 1)
                if t == 15:
                    with dve.If(more):
                        g_gate_up(cur.e + 1, 0)

        @block.gpsimd
        def _(pool):
            sub = ALU.subtract

            pool.wait_ge(boot_hi, 3)
            pool.tensor_tensor(GWs[:, :, E:2 * E], raw[:, BGW:BSG].rearrange("p (k m) -> p k m", k=KH),
                               f32(GWs[:, :, 0:E]), sub).then_inc(boot_lo, 1)

            def condition(c):
                for k in range(KH):
                    pool.wait_ge(q_ok, 1)
                    pool.wait_ge(xsum_ok, c + 1)
                    v = xc[:, k, :].rearrange("p (b s) -> p b s", s=SEQ)
                    qc = q[:, k, bass.ds(chunk(c) * CB, CB)].unsqueeze(2).broadcast_to([P, CB, SEQ])
                    last = pool.tensor_tensor(v, v, qc, ALU.mult)
                last.then_inc(xc_ok, 1)
                pool.wait_ge(xc_hi, c + 1)
                pool.tensor_tensor(xcs[:, 1], xc, f32(xcs[:, 0]), sub).then_inc(xc_lo, 1)

            def h_low(c):
                pool.wait_ge(h_hi, c + 1)
                cols = bass.ds(chunk(c) * CH, CH)
                pool.tensor_tensor(hs[:, 1, :, cols], hf, f32(hs[:, 0, :, cols]), sub).then_inc(h_lo, 1)

            condition(0)
            pool.tensor_tensor(SGs[:, 1].rearrange("p k m -> p (k m)"), raw[:, BSG:BSD],
                               f32(SGs[:, 0].rearrange("p k m -> p (k m)")), sub).then_inc(boot_lo, 1)
            pool.wait_ge(boot_hi, 4)
            pool.tensor_tensor(SDs[:, 1].rearrange("p b m -> p (b m)"), SDraw,
                               f32(SDs[:, 0].rearrange("p b m -> p (b m)")), sub).then_inc(boot_lo, 1)
            h_low(0)
            with pool.Fori(0, NCH) as c:
                for b in range(3):
                    n = SB[b][1]
                    pool.wait_ge(s_ahi, c * 3 + b + 1)
                    pool.tensor_tensor(hSs[0:n, b, 1, :], mS[0:n, :], f32(hSs[0:n, b, 0, :]), sub).then_inc(s_alo, 1)
                    if b == 1:
                        with pool.If(c < NCH - 1):
                            condition(c + 1)
                with pool.If(c < NCH - 1):
                    h_low(c + 1)
                pool.wait_ge(s_hi, c + 1)
                pool.wait_ge(soft_out, c * 64)
                pool.tensor_tensor(sfs[0:E, 1, :], sTs[0:E, :], f32(sfs[0:E, 0, :]), sub).then_inc(s_lo, 1)

            def fold(e):
                pool.wait_ge(raw_in, e * 32 + 32)
                pool.tensor_tensor(raw[:, QB:QB + QW], raw[:, QB:QB + QW], scb[:, 0:QW], ALU.mult).then_inc(foldQ, 1)
                r = raw[0:KR, DN + H:DN + 2 * H]
                pool.tensor_tensor(r, r, scb[0:KR, QW:QW + H], ALU.mult).then_inc(foldR, 1)

            def piece(e, wp, z, before):
                cols = bass.ds(z * PW, PW)
                pool.wait_ge(foldQ, e + 1)
                pool.wait_ge(foldR, e + 1)
                if before is not None:
                    pool.wait_ge(y_mm[1], before)
                pool.tensor_copy(Wt[wp][:, 0, cols], raw[:, cols]).then_inc(piece_hi, 1)
                pool.wait_ge(piece_hi, e * PIECES + z + 1)
                pool.tensor_tensor(Wt[wp][:, 1, cols], raw[:, cols], f32(Wt[wp][:, 0, cols]), sub).then_inc(piece_lo, 1)

            def adapter_weights(e, wp):
                src = raw[:, ADR:MU].rearrange("p (k m) -> p k m", k=2)
                pool.tensor_copy(ADt[:, wp, :, 0:KR], src).then_inc(adw_hi, 1)
                pool.wait_ge(adw_hi, e + 1)
                pool.tensor_tensor(ADt[:, wp, :, KR:P], src, f32(ADt[:, wp, :, 0:KR]), sub).then_inc(adw_lo, 1)

            fold(0)
            with pool.Fori(0, PIECES) as z:
                piece(0, 0, z, None)
            adapter_weights(0, 0)
            pool.wait_ge(sy_add, NCH)
            for p in (0, 1):
                pool.memset(f32(Xu[p][0:KR, :]), 0.0).then_inc(zeros_ok, 1)
            pool.memset(mC, 0.0).then_inc(zeros_ok, 1)
            pool.wait_ge(zeros_ok, 3)
            for prev, cur, nxt, (t, j), more in steps(pool):
                with when(pool, t, (16,), more):
                    pool.wait_ge(scl_in[cur.p], cur.same * 16 + 16)
                    pool.wait_ge(mulA[cur.p], cur.now)
                    pool.tensor_tensor(mA, mA, scl[cur.p], ALU.mult).then_inc(scA[cur.p], 1)
                    pool.wait_ge(mulC[cur.p], cur.now)
                    pool.tensor_tensor(mC, mC, scl[cur.p], ALU.mult).then_inc(scC[cur.p], 1)
                if t == 0:
                    fold(1)
                if t in (8, 16):
                    with pool.If(more):
                        fold(cur.e + 1)
                if j is not None:
                    with when(pool, t, (9, 10), more):
                        piece(cur.e + 1, 1 - cur.w, j * 2 + (t - 1) % NCH, cur.e * (NCH // 2))
                if t == 7:
                    adapter_weights(cur.e + 1, 1)
                if t == 15:
                    with pool.If(more):
                        adapter_weights(cur.e + 1, 0)


def kernel(x, cond_1024, L0_cond_W3, L0_cond_b3, L0_cond_W2, L0_cond_b2, L0_ffn_gate_weight, L0_ffn_inv_mapping,
           L0_ffn_mask_up_W, L0_ffn_gate_W, L0_ffn_gate_qa, L0_ffn_gate_qb, L0_ffn_gate_scale, L0_ffn_up_W,
           L0_ffn_up_qa, L0_ffn_up_qb, L0_ffn_up_scale, L0_ffn_down_W, L0_ffn_down_qa, L0_ffn_down_qb,
           L0_ffn_down_scale, L0_ffn_sh_gate_W, L0_ffn_sh_up_W, L0_ffn_sh_down_W):
    import numpy as np
    import concourse.bacc as bacc
    from concourse.bass_utils import run_bass_kernel_spmd as run

    f = np.float32

    def tiles(a):
        return a.reshape(-1, P, a.shape[-1]).transpose(1, 0, 2)

    def T(a):
        return np.swapaxes(np.asarray(a), -1, -2)

    def rk(a):
        return np.asarray(a).transpose(0, 3, 1, 2).reshape(F, KR, a.shape[2])

    x = np.asarray(x)
    xT = tiles(T(x.reshape(TOKENS, H)))
    boot = np.zeros((P, BOOT), f)
    boot[:, BW2:BGW] = tiles(np.asarray(L0_cond_W2)).reshape(P, -1)
    boot[:, BGW:BSG] = tiles(T(L0_ffn_gate_weight)).reshape(P, -1)
    sgT, suT, sd = tiles(T(L0_ffn_sh_gate_W)), tiles(T(L0_ffn_sh_up_W)), T(L0_ffn_sh_down_W)
    boot[:, BSG:BSD] = np.concatenate([w[:, :, at:at + n] for at, n in SB for w in (sgT, suT)], axis=2).reshape(P, -1)
    for b, (at, n) in enumerate(SB):
        boot[0:n, BSD + b * H:BSD + (b + 1) * H] = sd[at:at + n]

    raw = np.zeros((F, P, RAWW), f)
    gW, uW = (T(w).reshape(F, KH, P, I) for w in (L0_ffn_gate_W, L0_ffn_up_W))
    qa = [rk(np.swapaxes(np.asarray(w), 2, 3)).transpose(0, 2, 1).reshape(F, KH, P, KR)
          for w in (L0_ffn_gate_qa, L0_ffn_up_qa)]
    mu = np.asarray(L0_ffn_mask_up_W).reshape(F, KH, P, K)
    for k in range(KH):
        o = k * XW
        raw[:, :, o + XA:o + XA + KR] = qa[0][:, k]
        raw[:, :, o + XA + KR:o + XA + P] = qa[1][:, k]
        raw[:, :, o + XGA:o + XGA + P] = gW[:, k, :, 0:P]
        raw[:, :, o + XC:o + XC + TAIL] = gW[:, k, :, P:I]
        raw[:, :, o + XC + KR:o + XC + CW] = uW[:, k, :, P:I]
        raw[:, :, o + XUB:o + XUB + P] = uW[:, k, :, 0:P]
        for row in (0, KR):
            for part in range(3):
                at = MU + k * P + row + part * K
                raw[:, :, at:at + K] = mu[:, k]
    gq, uq = (rk(w) for w in (L0_ffn_gate_qb, L0_ffn_up_qb))
    scale = np.zeros((F, QW + H), f)
    gs, us = np.asarray(L0_ffn_gate_scale), np.asarray(L0_ffn_up_scale)
    for half in (0, KR):
        rows = slice(half, half + KR)
        raw[:, rows, QGA:QGA + P] = gq[:, :, 0:P]
        raw[:, rows, QGC:QGC + TAIL] = gq[:, :, P:I]
        raw[:, rows, QUB:QUB + P] = uq[:, :, 0:P]
        raw[:, rows, QUC + KR:QUC + CW] = uq[:, :, P:I]
    scale[:, QGA - QB:QGA - QB + P] = gs[:, 0:P]
    scale[:, QGC - QB:QGC - QB + TAIL] = gs[:, P:I]
    scale[:, QUB - QB:QUB - QB + P] = us[:, 0:P]
    scale[:, QUC - QB + KR:QUC - QB + CW] = us[:, P:I]
    scale[:, QW:] = np.asarray(L0_ffn_down_scale)
    dW = T(L0_ffn_down_W)
    raw[:, :, DN:DN + H] = dW[:, 0:P]
    raw[:, 0:KR, DN + H:DN + 2 * H] = rk(L0_ffn_down_qb)
    raw[:, KR:CW, DN + H:DN + 2 * H] = dW[:, P:I]
    da = rk(np.swapaxes(np.asarray(L0_ffn_down_qa), 2, 3)).transpose(0, 2, 1)
    raw[:, :, ADR:ADR + KR] = da[:, 0:P]
    raw[:, KR:CW, ADR + KR:ADR + 2 * KR] = da[:, P:I]

    consts = np.zeros((P, CONSTS), f)
    consts[:, 0:P] = np.eye(P)
    for row in (0, KR):
        consts[row + 2 * K:row + 3 * K, P] = -1.0
    consts[:, P + 1] = np.arange(P)
    consts[:, P + 2] = np.arange(P) - E
    vecs = np.concatenate([np.asarray(v).reshape(KH, P).T for v in (L0_cond_b3, L0_cond_b2)], axis=1)

    arrays = {
        "xT": xT, "condT": T(cond_1024), "W3": np.asarray(L0_cond_W3), "vecs": vecs, "consts": consts,
        "inv": np.asarray(L0_ffn_inv_mapping), "boot": boot, "raw": raw.reshape(F * P, RAWW), "scale": scale,
    }
    arrays = {"in_" + n: np.ascontiguousarray(a) for n, a in arrays.items()}
    nc = bacc.Bacc("TRN2", target_bir_lowering=False, num_devices=1)
    args = [nc.dram_tensor(n, a.shape, mybir.dt.from_np(a.dtype), kind="ExternalInput").ap() for n, a in arrays.items()]
    out = nc.dram_tensor("out_T", (P, KH, TOKENS), F32, kind="ExternalOutput").ap()
    build(nc, *args, out)
    got = run(nc, [arrays], core_ids=[0]).results[0]["out_T"]
    return got.transpose(2, 1, 0).reshape(BATCH, SEQ, H)
```

```python
from contextlib import ExitStack, nullcontext

import concourse.bass as bass
from concourse import mybir

F32 = mybir.dt.float32
F32R = mybir.dt.float32r
I32 = mybir.dt.int32
ALU = mybir.AluOpType
ACT = mybir.ActivationFunctionType
AX = mybir.AxisListType.X

P = 128
BATCH, SEQ, H, COND = 128, 32, 256, 128
TOKENS = BATCH * SEQ
CH = 512
NCH = TOKENS // CH
CB = CH // SEQ
TT = CH // P
KH = H // P
E, F, K, R, TOPK = 64, 8, 8, 8, 6
KR = K * R
I = 176
TAIL = I - P
CW = KR + TAIL
ISH = 2 * I
SB = [(0, P), (P, P), (2 * P, ISH - 2 * P)]

XA, XGA, XC, XUB, XW = 0, P, 2 * P, 2 * P + CW, 3 * P + CW
QB = KH * XW
QGA, QGC, QUC, QUB = QB, QB + P, QB + P + CW, QB + P + 2 * CW
QW = 2 * P + 2 * CW
DN = QB + QW
SPLIT = DN + 2 * H
PIECES = NCH - 2
PW = -(-SPLIT // (2 * PIECES)) * 2
SPLITW = PW * PIECES
ADR = SPLITW
MU = ADR + 2 * KR
RAWW = MU + KH * P
BW2, BGW, BSG, BSD = 0, KH * H, KH * H + KH * E, KH * H + KH * E + KH * 2 * ISH
BOOT = BSD + 3 * H
CONSTS = P + 3
NEG = -1.0e9
GONE = -3.0e38
ABSENT = 3.0e38


class Unit:

    def __init__(self, e, c, k, p, w):
        self.e, self.c, self.k, self.p, self.w = e, c, k, p, w
        self.now, self.last, self.same = k + 1, k + p, k


def steps(eng):
    def unit(i, t, j=0):
        return Unit(i * 2 + t // NCH, j * 2 + t % NCH, i * NCH + (j + t // 2), t % 2, (t // NCH) % 2)

    yield None, unit(0, 0), unit(0, 1), (0, None), None
    pairs = F // 2
    with eng.Fori(0, pairs) as i:
        for t0 in (0, NCH):
            with eng.Fori(0, (NCH - 2) // 2) as j:
                for t in (t0 + 1, t0 + 2):
                    yield unit(i, t - 1, j), unit(i, t, j), unit(i, t + 1, j), (t, j), i < pairs - 1
            for t in (t0 + NCH - 1, t0 + NCH):
                yield unit(i, t - 1), unit(i, t), unit(i, t + 1), (t, None), i < pairs - 1


def build(nc, xT, condT, W3, vecs, consts, inv, boot, raw_d, scale_d, outT):
    soft_d = nc.dram_tensor("soft_scratch", (NCH * (E + F), CH), F32, kind="Internal").ap()
    packed_d = nc.dram_tensor("packed_scratch", (NCH * 3 * E, CH), F32, kind="Internal").ap()

    with ExitStack() as ctx:
        def sb(name, cols, dt=F32):
            return ctx.enter_context(nc.sbuf_tensor(name, [P, cols], dt))

        def carve(arena, sizes):
            out, at = [], 0
            for n in sizes:
                out.append(arena[:, at:at + n])
                at += n
            assert at <= arena.shape[1], (at, arena.shape)
            return out

        y = sb("y", KH * TOKENS)[:, :].rearrange("p (k t) -> p k t", k=KH)
        hs = sb("h_split", 2 * KH * TOKENS, F32R)[:, :].rearrange("p (s k t) -> p s k t", s=2, k=KH)
        W_even = sb("W_even", 2 * SPLITW, F32R)
        ADt = sb("down_adapter", 2 * 2 * P, F32R)[:, :].rearrange("p (w k m) -> p w k m", w=2, k=2)
        A3 = sb("a_packed", 2 * P, F32R)[:, :].rearrange("p (w m) -> p w m", w=2)
        Gh = sb("G_hi", XW, F32R)
        raw = sb("raw", RAWW)
        scb = sb("scales", QW + H)
        q = sb("q_emb", KH * BATCH)[:, :].rearrange("p (k b) -> p k b", k=KH)
        cst = sb("consts", CONSTS)
        eye, lomask, rowno = cst[:, 0:P], cst[:, P:P + 1], cst[:, P + 1:P + 3]
        onehot = sb("onehot", 2 * E)
        vec = sb("vectors", 2 * KH)
        b3s, b2s = vec[:, 0:KH], vec[:, KH:2 * KH]

        RA = sb("arena_r", 16 * CH + 2 * SPLITW, F32R)
        FA = sb("arena_f", 13 * CH)

        (W2s, GWs, SGs, SDs, xcs, hSs, sfs) = carve(
            RA, [2 * KH * H, KH * 2 * E, 2 * KH * 2 * ISH, 2 * 3 * H, 2 * KH * CH, 3 * 2 * CH, 2 * CH])
        W2s = W2s.rearrange("p (s k m) -> p s k m", s=2, k=KH)
        GWs = GWs.rearrange("p (k m) -> p k m", k=KH)
        SGs = SGs.rearrange("p (s k m) -> p s k m", s=2, k=KH)
        SDs = SDs.rearrange("p (s b m) -> p s b m", s=2, b=3)
        xcs = xcs.rearrange("p (s k t) -> p s k t", s=2, k=KH)
        hSs = hSs.rearrange("p (b s t) -> p b s t", b=3, s=2)
        sfs = sfs.rearrange("p (s t) -> p s t", s=2)
        (xc_, hf_, RLs, lg, ex, rep, wsel, z, st, wTs, sTs, sS, mS, top, sm, rs, gm, gs, vs) = carve(
            FA, [KH * CH, KH * CH, CH, TT * E, TT * E, TT * E, TT * E, TT * E, TT * (E + F), TT * E, CH, CH, CH,
                 TT * 8, TT, TT, TT * F, TT * F, KH * CB])
        xc = xc_.rearrange("p (k t) -> p k t", k=KH)
        hf = hf_.rearrange("p (k t) -> p k t", k=KH)
        lg, ex, rep, wsel, z, st, top = (v.rearrange("p (j e) -> p j e", j=TT)
                                         for v in (lg, ex, rep, wsel, z, st, top))
        W3s, cTs, invs = xc_[:, 0:H], xc_[:, H:H + BATCH], z[:, 0, :].bitcast(I32)
        invf, invn = ex[:, 0, :], ex[:, 1, :]
        SDraw = hf_[:, 0:3 * H]

        r2 = carve(RA, [CH] * 16 + [2 * SPLITW])
        Vg, Vu, Xg, Xu, Ahi, Alo, Rhi, Rlo = (r2[2 * n:2 * n + 2] for n in range(8))
        Wt = [W_even[:, :].rearrange("p (s m) -> p s m", s=2), r2[16].rearrange("p (s m) -> p s m", s=2)]
        f2 = carve(FA, [CH] * 13)
        wexp, wdn, scl = (f2[2 * n:2 * n + 2] for n in range(3))
        ap, sA, sC, mA, mC, adc, adp = f2[6:13]

        PS = ctx.enter_context(nc.psum_tensor("ps", [P, 8, CH], F32))
        pA, pB, pC, pa, pad, pG = (PS[:, n, :] for n in range(6))
        pY = PS[:, 6:8, :]
        APK = slice(P - 32, P - 32 + 3 * K)
        TAILS = slice(KR, CW)

        def sem(name):
            return ctx.enter_context(nc.semaphore(name))

        def sems(names):
            return [sem(n) for n in names.split()]

        def pairs(names):
            return [[sem(n + "_even"), sem(n + "_odd")] for n in names.split()]

        (consts_in, x_in, boot_in, sd_in, raw_in, soft_out, y_out) = sems(
            "consts_in x_in boot_in sd_in raw_in soft_out y_out")
        (inv_f, inv_n, inv_w, inv_c, onehot_ok, q_mm, q_ok, boot_hi, w2_lo, boot_lo) = sems(
            "inv_f inv_n inv_w inv_c onehot_ok q_mm q_ok boot_hi w2_lo boot_lo")
        (vsum_ok, xsum_ok, xc_ok, xc_hi, xc_lo, h_mm, hf_ok, h_hi, h_lo, rl_mm, rl_cp, tl_mm, lg_ok) = sems(
            "vsum_ok xsum_ok xc_ok xc_hi xc_lo h_mm hf_ok h_hi h_lo rl_mm rl_cp tl_mm lg_ok")
        (top_ok, absent_ok, rep_ok, dl_ok, ex_ok, sm_ok, rs_ok, wsel_ok, wn_ok, wT_mm, wT_cp, fl_mm) = sems(
            "top_ok absent_ok rep_ok dl_ok ex_ok sm_ok rs_ok wsel_ok wn_ok wT_mm wT_cp fl_mm")
        (z_neg, z_all, tot_ok, gm_ok, z_sub, z_exp, gs_ok, gr_ok, soft_ok, sT_mm, sT_cp, s_hi, s_lo) = sems(
            "z_neg z_all tot_ok gm_ok z_sub z_exp gs_ok gr_ok soft_ok sT_mm sT_cp s_hi s_lo")
        (sg_mm, s_sil, s_mul, s_ahi, s_alo, sy_mm, sy_add) = sems("sg_mm s_sil s_mul s_ahi s_alo sy_mm sy_add")
        a_mm, gA_mm, gB_mm, gC_mm, ad_mm, y_mm = pairs("a_mm gA_mm gB_mm gC_mm ad_mm y_mm")
        ap_ok, vg_lo, vu_lo, ad_sum, adp_ok, ad_lo, mulA, loA, mulC, loC, y_add = pairs(
            "ap_ok vg_lo vu_lo ad_sum adp_ok ad_lo mulA loA mulC loC y_add")
        vg_hi, vu_hi, xg_hi, xu_hi, ad_cp, silA, ad_hi, hiA, silC, hiC = pairs(
            "vg_hi vu_hi xg_hi xu_hi ad_cp silA ad_hi hiA silC hiC")
        scA, scC, wexp_in, wdn_in, scl_in, pk_in, pka_in = pairs("scA scC wexp_in wdn_in scl_in pk_in pka_in")
        (foldQ, foldR, piece_hi, piece_lo, adw_hi, adw_lo, g_mm, g_hi, a3_ok, g3g_ok, g3u_ok, zeros_ok) = sems(
            "foldQ foldR piece_hi piece_lo adw_hi adw_lo g_mm g_hi a3_ok g3g_ok g3u_ok zeros_ok")

        def f32(v):
            return v.bitcast(F32)

        def when(eng, t, steps_, cond):
            return eng.If(cond) if t in steps_ else nullcontext()

        def real(e):
            if isinstance(e, int):
                return e
            return nc.s_assert_within(e, 0, F - 1, skip_runtime_bounds_check_because="left out in the last pair")

        def chunks(eng, body):
            body(0, True, False)
            with eng.Fori(1, NCH - 1) as c:
                body(c, False, False)
            body(NCH - 1, False, True)

        block = ctx.enter_context(nc.Block())

        @block.sync
        def _(sp):
            sp.dma_start(y[:, :, 0:CH], xT[:, :, 0:CH]).then_inc(x_in, 16)
            sp.dma_start(raw[:, 0:BSD], boot[:, 0:BSD]).then_inc(boot_in, 16)
            sp.dma_start(SDraw, boot[:, BSD:BOOT]).then_inc(sd_in, 16)
            with sp.Fori(1, NCH) as c:
                sp.wait_ge(x_in, c * 16)
                sp.dma_start(y[:, :, bass.ds(c * CH, CH)], xT[:, :, bass.ds(c * CH, CH)]).then_inc(x_in, 16)

            def load_split(e):
                e = real(e)
                sp.dma_start(raw[:, 0:SPLITW], raw_d[bass.ds(e * P, P), 0:SPLITW]).then_inc(raw_in, 16)
                row = scale_d[bass.ds(e, 1), :]
                sp.dma_start(scb[:, :], bass.AP(row.tensor, row.offset, [[0, P], [1, QW + H]])).then_inc(raw_in, 16)

            def load_rest(e):
                sp.dma_start(raw[:, ADR:RAWW], raw_d[bass.ds(real(e) * P, P), ADR:RAWW]).then_inc(raw_in, 16)

            sp.wait_ge(boot_hi, 4)
            sp.wait_ge(w2_lo, 1)
            sp.wait_ge(boot_lo, 3)
            load_split(0)
            load_rest(0)

            def store(c):
                sp.wait_ge(sT_cp, c + 1)
                sp.dma_start(soft_d[bass.ds(c * (E + F), E + F), :], sTs[0:E + F, :]).then_inc(soft_out, 16)
                sp.wait_ge(s_hi, c + 1)
                sp.dma_start(packed_d[bass.ds(c * 3 * E, E), :], f32(sfs[0:E, 0, :])).then_inc(soft_out, 16)
                sp.dma_start(packed_d[bass.ds(c * 3 * E + 2 * E, E), :], f32(sfs[0:E, 0, :])).then_inc(soft_out, 16)
                sp.wait_ge(s_lo, c + 1)
                sp.dma_start(packed_d[bass.ds(c * 3 * E + E, E), :], f32(sfs[0:E, 1, :])).then_inc(soft_out, 16)

            with sp.Fori(0, NCH - 1) as c:
                store(c)

            def load_unit(n):
                e = real(n.e)
                row = soft_d[bass.ds(n.c * (E + F) + e * K, K), :]
                part = packed_d[bass.ds(n.c * 3 * E + e * K, K), :]
                total = soft_d[bass.ds(n.c * (E + F) + e + E, 1), :]
                packed = bass.AP(part.tensor, part.offset, [[E * CH, 3], [CH, K], [1, CH]])
                sp.wait_ge(a_mm[n.p], n.same)
                sp.dma_start(f32(Xg[n.p][APK, :]), packed).then_inc(pka_in[n.p], 16)
                sp.wait_ge(ap_ok[n.p], n.same)
                sp.dma_start(wexp[n.p], bass.AP(row.tensor, row.offset, [[0, 2 * R], [CH, K], [1, CH]])
                             ).then_inc(wexp_in[n.p], 16)
                sp.wait_ge(gB_mm[n.p], n.same)
                sp.dma_start(f32(Xu[n.p][0:3 * K, :]), packed).then_inc(pk_in[n.p], 16)
                sp.dma_start(f32(Xg[n.p][KR:KR + 3 * K, :]), packed).then_inc(pk_in[n.p], 16)
                sp.wait_ge(scA[n.p], n.same)
                sp.wait_ge(scC[n.p], n.same)
                sp.dma_start(scl[n.p], bass.AP(total.tensor, total.offset, [[0, P], [1, CH]])
                             ).then_inc(scl_in[n.p], 16)
                sp.wait_ge(adp_ok[n.p], n.same)
                sp.dma_start(wdn[n.p][0:KR, :], bass.AP(row.tensor, row.offset, [[0, R], [CH, K], [1, CH]])
                             ).then_inc(wdn_in[n.p], 16)

            def next_split(e):
                sp.wait_ge(piece_hi, e * PIECES)
                sp.wait_ge(piece_lo, e * PIECES)
                sp.wait_ge(g_mm, e)
                load_split(e)

            def next_rest(e):
                sp.wait_ge(adw_hi, e)
                sp.wait_ge(adw_lo, e)
                load_rest(e)

            for prev, cur, nxt, (t, _j), more in steps(sp):
                if prev is None:
                    sp.wait_ge(soft_out, 64 * (NCH - 1))
                    sp.wait_ge(sg_mm, 3 * NCH)
                    sp.wait_ge(wn_ok, NCH)
                    sp.wait_ge(zeros_ok, 2)
                    load_unit(cur)
                    load_unit(nxt)
                    store(NCH - 1)
                    sp.wait_ge(soft_out, 64 * NCH)
                    next_split(1)
                    next_rest(1)
                    continue
                with when(sp, t, (15, 16), more):
                    load_unit(nxt)
                if t in (7, 15):
                    with sp.If(more):
                        next_split(cur.e + 2)
                if t in (8, 16):
                    with sp.If(more):
                        next_rest(cur.e + 1)
            with sp.Fori(0, NCH // 2) as c:
                for p in (0, 1):
                    sp.wait_ge(y_add[p], c + ((F - 1) * NCH // 2 + 1))
                    sp.dma_start(outT[:, :, bass.ds((c * 2 + p) * CH, CH)], y[:, :, bass.ds((c * 2 + p) * CH, CH)]
                                 ).then_inc(y_out, 16)
            sp.wait_ge(y_out, 16 * NCH)

        @block.tensor
        def _(pe):
            def product(out, parts, first=True, last=True):
                for n, (lhsT, rhs) in enumerate(parts):
                    mm = pe.matmul(out, lhsT, rhs, start=first and n == 0, stop=last and n == len(parts) - 1)
                return mm

            def three(w_hi, w_lo, v_hi, v_lo):
                return [(w_hi, v_hi), (w_lo, v_hi), (w_hi, v_lo)]

            pe.wait_ge(consts_in, 16 * 5)
            for m in range(KH):
                mm = product(PS[:, 2, m * BATCH:(m + 1) * BATCH], [(W3s[:, m * P:(m + 1) * P], cTs)])
            mm.then_inc(q_mm, 1)

            def h_products(c):
                pe.wait_ge(xc_hi, c + 1)
                pe.wait_ge(xc_lo, c + 1)
                pe.wait_ge(hf_ok, c)
                for m in range(KH):
                    ms = slice(m * P, (m + 1) * P)
                    mm = product(PS[:, m, :], [x for k in range(KH) for x in
                                               three(W2s[:, 0, k, ms], W2s[:, 1, k, ms], xcs[:, 0, k, :], xcs[:, 1, k, :])])
                mm.then_inc(h_mm, 1)

            def h_of(c):
                return [[hs[:, s, k, bass.ds(c * CH, CH)] for k in range(KH)] for s in (0, 1)]

            pe.wait_ge(boot_hi, 1)
            pe.wait_ge(w2_lo, 1)
            pe.wait_ge(onehot_ok, 1)
            h_products(0)
            pe.wait_ge(boot_hi, 4)
            pe.wait_ge(boot_lo, 3)

            def shared_up(c, b):
                at, n = SB[b]
                hh, hl = h_of(c)
                pe.wait_ge(s_mul, c * 3 + b)
                for g in (0, 1):
                    ms = slice(2 * at + g * n, 2 * at + (g + 1) * n)
                    mm = product(PS[0:n, 4 + g, :], [x for k in range(KH) for x in
                                                     three(SGs[:, 0, k, ms], SGs[:, 1, k, ms], hh[k], hl[k])])
                mm.then_inc(sg_mm, 1)

            def shared_down(c, b):
                n = SB[b][1]
                pe.wait_ge(s_ahi, c * 3 + b + 1)
                pe.wait_ge(s_alo, c * 3 + b + 1)
                if b == 0:
                    pe.wait_ge(sy_add, c)
                for m in range(KH):
                    ms = slice(m * P, (m + 1) * P)
                    mm = product(PS[:, 6 + m, :], three(SDs[0:n, 0, b, ms], SDs[0:n, 1, b, ms],
                                                        hSs[0:n, b, 0, :], hSs[0:n, b, 1, :]),
                                 first=b == 0, last=b == 2)
                mm.then_inc(sy_mm, 1)

            def gather(c):
                pe.wait_ge(wT_cp, c + 1)
                for j in range(TT // 2):
                    mm = product(PS[:, 3, (TT // 2 + j) * P:(TT // 2 + j + 1) * P],
                                 [(wTs[:, j * P:(j + 1) * P], onehot[:, :])])
                mm.then_inc(fl_mm, 1)

            def groups_to_rows(c):
                pe.wait_ge(soft_ok, c + 1)
                pe.wait_ge(tot_ok, c + 1)
                for j in range(TT):
                    mm = pe.transpose(PS[0:E + F, 2, j * P:(j + 1) * P], st[:, j, :], eye)
                mm.then_inc(sT_mm, 1)

            def phase1(c, first, last):
                hh, hl = h_of(c)
                pe.wait_ge(h_hi, c + 1)
                pe.wait_ge(h_lo, c + 1)
                if not first:
                    pe.wait_ge(sT_cp, c - 1)
                product(PS[:, 2, :], [(GWs[:, k, :], v[k]) for k in range(KH) for v in (hh, hl)]).then_inc(rl_mm, 1)
                shared_up(c, 0)
                if not first:
                    gather(c - 1)
                    shared_down(c - 1, 2)
                pe.wait_ge(rl_cp, c + 1)
                pe.wait_ge(tot_ok, c)
                pe.wait_ge(z_all, c)
                for j in range(TT):
                    mm = pe.transpose(PS[:, 3, j * P:(j + 1) * P], RLs[:, j * P:(j + 1) * P], eye)
                mm.then_inc(tl_mm, 1)
                shared_up(c, 1)
                if not last:
                    h_products(c + 1)
                shared_up(c, 2)
                shared_down(c, 0)
                if not first:
                    groups_to_rows(c - 1)
                shared_down(c, 1)
                pe.wait_ge(wn_ok, c + 1)
                pe.wait_ge(lg_ok, c + 1)
                for j in range(TT // 2):
                    mm = pe.transpose(PS[:, 3, j * P:(j + 1) * P], wsel[:, 2 * j:2 * j + 2, :], eye)
                mm.then_inc(wT_mm, 1)

            chunks(pe, phase1)

            def w(n, s, at, width=P, rows=slice(0, P)):
                return Wt[n.w][rows, s, at:at + width]

            def from_h(n, at, width=P):
                hh, hl = h_of(n.c)
                return [x for k in range(KH) for x in
                        three(w(n, 0, k * XW + at, width), w(n, 1, k * XW + at, width), hh[k], hl[k])]

            def g_products(e):
                pe.wait_ge(raw_in, e * 48 + 48)
                pe.wait_ge(a3_ok, e)
                pe.wait_ge(g3g_ok, e)
                pe.wait_ge(g3u_ok, e)
                product(pG[:, 0:XW], [(raw[:, MU + k * P:MU + (k + 1) * P], raw[:, k * XW:(k + 1) * XW])
                                      for k in range(KH)]).then_inc(g_mm, 1)

            def adapters_in(n, fresh):
                if fresh:
                    pe.wait_ge(piece_hi, n.e * PIECES + PIECES)
                    pe.wait_ge(piece_lo, n.e * PIECES + PIECES)
                    pe.wait_ge(a3_ok, n.e + 1)
                pe.wait_ge(ap_ok[1 - n.p], n.last)
                product(pa, from_h(n, XA), last=False)
                pe.wait_ge(pka_in[n.p], n.same * 16 + 16)
                product(pa, [(A3[APK, n.w, :], Xg[n.p][APK, :])], first=False).then_inc(a_mm[n.p], 1)

            def down_adapter(n, fresh):
                if fresh:
                    pe.wait_ge(adw_hi, n.e + 1)
                    pe.wait_ge(adw_lo, n.e + 1)
                pe.wait_ge(hiA[n.p], n.now)
                pe.wait_ge(loA[n.p], n.now)
                pe.wait_ge(hiC[n.p], n.now)
                pe.wait_ge(loC[n.p], n.now)
                pe.wait_ge(ad_sum[1 - n.p], n.last)
                product(pad, [(ADt[:, n.w, 0, :], Ahi[n.p]), (ADt[:, n.w, 0, :], Alo[n.p]),
                              (ADt[TAILS, n.w, 1, :], Rhi[n.p][TAILS, :]),
                              (ADt[TAILS, n.w, 1, :], Rlo[n.p][TAILS, :])]).then_inc(ad_mm[n.p], 1)

            def gate_up(n, fresh):
                packed = slice(0, KR + 3 * K)
                if fresh:
                    pe.wait_ge(g3g_ok, n.e + 1)
                    pe.wait_ge(g3u_ok, n.e + 1)
                pe.wait_ge(mulC[1 - n.p], n.last)
                product(pC[0:CW, :], from_h(n, XC, CW), last=False)
                pe.wait_ge(vg_hi[n.p], n.now)
                pe.wait_ge(vg_lo[n.p], n.now)
                pe.wait_ge(xg_hi[n.p], n.now)
                pe.wait_ge(vu_hi[n.p], n.now)
                pe.wait_ge(vu_lo[n.p], n.now)
                pe.wait_ge(xu_hi[n.p], n.now)
                pe.wait_ge(pk_in[n.p], n.same * 32 + 32)
                up = slice(KR, P)
                product(pC[0:CW, :], [
                    (w(n, 0, QGC, CW), Vg[n.p]), (w(n, 1, QGC, CW, packed), Xg[n.p][packed, :]),
                    (w(n, 0, QUC, CW), Vu[n.p]), (w(n, 1, QUC, CW, up), Xu[n.p][up, :])],
                    first=False).then_inc(gC_mm[n.p], 1)
                pe.wait_ge(silA[1 - n.p], n.last)
                product(pA, from_h(n, XGA) + [(w(n, 0, QGA), Vg[n.p]), (w(n, 1, QGA, P, packed), Xg[n.p][packed, :])]
                        ).then_inc(gA_mm[n.p], 1)
                pe.wait_ge(mulA[1 - n.p], n.last)
                product(pB, from_h(n, XUB) + [(w(n, 0, QUB), Vu[n.p]), (w(n, 1, QUB), Xu[n.p])]
                        ).then_inc(gB_mm[n.p], 1)

            def down(n):
                pe.wait_ge(ad_hi[n.p], n.now)
                pe.wait_ge(ad_lo[n.p], n.now)
                pe.wait_ge(y_add[1 - n.p], n.last)
                r = slice(0, CW)
                for m in range(KH):
                    dA, dR = DN + m * P, DN + H + m * P
                    mm = product(pY[:, m, :], three(w(n, 0, dA), w(n, 1, dA), Ahi[n.p], Alo[n.p]) +
                                 three(w(n, 0, dR, P, r), w(n, 1, dR, P, r), Rhi[n.p][r, :], Rlo[n.p][r, :]))
                mm.then_inc(y_mm[n.p], 1)

            pe.wait_ge(s_mul, 3 * NCH)
            g_products(0)
            gather(NCH - 1)
            shared_down(NCH - 1, 2)
            for prev, cur, nxt, (t, _j), more in steps(pe):
                if prev is None:
                    pe.wait_ge(z_all, NCH)
                    pe.wait_ge(tot_ok, NCH)
                    adapters_in(cur, True)
                    groups_to_rows(NCH - 1)
                    adapters_in(nxt, False)
                    pe.wait_ge(sT_cp, NCH)
                    gate_up(cur, True)
                    g_products(1)
                    continue
                with when(pe, t, (15, 16), more):
                    adapters_in(nxt, t in (7, 15))
                down_adapter(prev, t in (1, 9))
                with when(pe, t, (16,), more):
                    gate_up(cur, t in (8, 16))
                down(prev)
                if t in (8, 16):
                    with pe.If(more):
                        g_products(cur.e + 1)

        @block.scalar
        def _(act):
            def copy(out, in_):
                return act.activation(out, in_, ACT.Copy)

            act.dma_start(W3s, W3).then_inc(consts_in, 16)
            act.dma_start(cTs, condT).then_inc(consts_in, 16)
            act.dma_start(vec[:, :], vecs).then_inc(consts_in, 16)
            act.dma_start(cst[:, :], consts).then_inc(consts_in, 16)
            act.dma_start(invs, bass.AP(inv.tensor, 0, [[0, P], [1, E]])).then_inc(consts_in, 16)

            act.wait_ge(boot_in, 16)
            copy(W2s[:, 0].rearrange("p k m -> p (k m)"), raw[:, BW2:BGW]).then_inc(boot_hi, 1)
            copy(GWs[:, :, 0:E], raw[:, BGW:BSG].rearrange("p (k m) -> p k m", k=KH)).then_inc(boot_hi, 1)
            copy(SGs[:, 0].rearrange("p k m -> p (k m)"), raw[:, BSG:BSD]).then_inc(boot_hi, 1)

            def condition_high(c):
                act.wait_ge(xc_ok, c + 1)
                act.wait_ge(h_mm, c)
                copy(xcs[:, 0], xc).then_inc(xc_hi, 1)

            def h_high(c):
                act.wait_ge(h_mm, c + 1)
                act.wait_ge(h_hi, c)
                act.wait_ge(h_lo, c)
                for m in range(KH):
                    last = act.activation(hf[:, m, :], PS[:, m, :], ACT.Relu, bias=b2s[:, m:m + 1])
                last.then_inc(hf_ok, 1)
                act.wait_ge(hf_ok, c + 1)
                copy(hs[:, 0, :, bass.ds(c * CH, CH)], hf).then_inc(h_hi, 1)

            condition_high(0)
            act.wait_ge(sd_in, 16)
            copy(SDs[:, 0].rearrange("p b m -> p (b m)"), SDraw).then_inc(boot_hi, 1)
            act.wait_ge(boot_hi, 4)
            act.wait_ge(boot_lo, 3)
            h_high(0)

            def shared_silu(c, b):
                n = SB[b][1]
                act.wait_ge(sg_mm, c * 3 + b + 1)
                act.wait_ge(s_mul, c * 3 + b)
                act.activation(sS[0:n, :], PS[0:n, 4, :], ACT.Silu).then_inc(s_sil, 1)

            def shared_high(c, b, first):
                n = SB[b][1]
                act.wait_ge(s_mul, c * 3 + b + 1)
                if not first:
                    act.wait_ge(sy_mm, c * 3 + b - 2)
                copy(hSs[0:n, b, 0, :], mS[0:n, :]).then_inc(s_ahi, 1)

            def routed_rows(c):
                act.wait_ge(wT_mm, c + 1)
                act.wait_ge(fl_mm, c)
                copy(wTs, PS[:, 3, 0:TT * E]).then_inc(wT_cp, 1)

            def groups_exp(c):
                act.wait_ge(z_sub, c + 1)
                act.activation(z, z, ACT.Exp).then_inc(z_exp, 1)

            def group_rows(c):
                act.wait_ge(sT_mm, c + 1)
                act.wait_ge(soft_out, c * 64)
                act.wait_ge(s_lo, c)
                copy(sTs[0:E + F, :], PS[0:E + F, 2, :]).then_inc(sT_cp, 1)

            def group_rows_high(c):
                act.wait_ge(sT_cp, c + 1)
                copy(sfs[0:E, 0, :], sTs[0:E, :]).then_inc(s_hi, 1)

            def phase1(c, first, last):
                act.wait_ge(rl_mm, c + 1)
                act.wait_ge(tl_mm, c)
                copy(RLs, PS[:, 2, :]).then_inc(rl_cp, 1)
                if not first:
                    routed_rows(c - 1)
                shared_silu(c, 0)
                if not last:
                    condition_high(c + 1)
                shared_high(c, 0, first)
                shared_silu(c, 1)
                act.wait_ge(dl_ok, c + 1)
                act.activation(ex, ex, ACT.Exp).then_inc(ex_ok, 1)
                if not first:
                    groups_exp(c - 1)
                shared_high(c, 1, first)
                if not last:
                    h_high(c + 1)
                shared_silu(c, 2)
                if not first:
                    group_rows(c - 1)
                shared_high(c, 2, first)
                if not first:
                    group_rows_high(c - 1)

            chunks(act, phase1)
            routed_rows(NCH - 1)

            def g_high(e):
                act.wait_ge(g_mm, e + 1)
                act.wait_ge(a3_ok, e)
                act.wait_ge(g3g_ok, e)
                act.wait_ge(g3u_ok, e)
                copy(Gh[:, :], pG[:, 0:XW]).then_inc(g_hi, 1)

            def adapters_high(n):
                g, u = slice(0, KR), slice(KR, P)
                act.wait_ge(ap_ok[n.p], n.now)
                act.wait_ge(gB_mm[n.p], n.same)
                copy(Vg[n.p][g, :], ap[g, :]).then_inc(vg_hi[n.p], 1)
                copy(Vu[n.p][u, :], ap[u, :]).then_inc(vu_hi[n.p], 1)

            def adapters_high_again(n):
                g, u = slice(0, KR), slice(KR, P)
                copy(Xg[n.p][g, :], ap[g, :]).then_inc(xg_hi[n.p], 1)
                copy(Xu[n.p][u, :], ap[u, :]).then_inc(xu_hi[n.p], 1)

            g_high(0)
            groups_exp(NCH - 1)
            for prev, cur, nxt, (t, _j), more in steps(act):
                if prev is None:
                    act.wait_ge(sg_mm, 3 * NCH)
                    adapters_high(cur)
                    adapters_high_again(cur)
                    group_rows(NCH - 1)
                    group_rows_high(NCH - 1)
                else:
                    act.wait_ge(ad_mm[prev.p], prev.now)
                    act.wait_ge(ad_sum[1 - prev.p], prev.last)
                    copy(adc[0:KR, :], pad[KR:P, :]).then_inc(ad_cp[prev.p], 1)
                with when(act, t, (15, 16), more):
                    adapters_high(nxt)
                if prev is not None:
                    act.wait_ge(adp_ok[prev.p], prev.now)
                    act.wait_ge(y_mm[prev.p], prev.same)
                    copy(Rhi[prev.p][0:KR, :], adp[0:KR, :]).then_inc(ad_hi[prev.p], 1)
                if prev is None:
                    act.wait_ge(zeros_ok, 3)
                with when(act, t, (16,), more):
                    act.wait_ge(gC_mm[cur.p], cur.now)
                    act.wait_ge(mulC[1 - cur.p], cur.last)
                    act.activation(sC[TAILS, :], pC[0:TAIL, :], ACT.Silu).then_inc(silC[cur.p], 1)
                with when(act, t, (15, 16), more):
                    adapters_high_again(nxt)
                with when(act, t, (16,), more):
                    act.wait_ge(gA_mm[cur.p], cur.now)
                    act.wait_ge(mulA[1 - cur.p], cur.last)
                    act.activation(sA, pA, ACT.Silu).then_inc(silA[cur.p], 1)
                    act.wait_ge(mulC[cur.p], cur.now)
                    act.wait_ge(y_mm[cur.p], cur.same)
                    copy(Rhi[cur.p][TAILS, :], mC[TAILS, :]).then_inc(hiC[cur.p], 1)
                    act.wait_ge(mulA[cur.p], cur.now)
                    copy(Ahi[cur.p], mA).then_inc(hiA[cur.p], 1)
                if prev is None:
                    g_high(1)
                if t in (8, 16):
                    with act.If(more):
                        g_high(cur.e + 1)

        @block.vector
        def _(dve):
            sub = ALU.subtract

            dve.wait_ge(consts_in, 16 * 5)
            dve.tensor_copy(invf, invs).then_inc(inv_f, 1)
            dve.wait_ge(inv_f, 1)
            dve.tensor_scalar(invn, invf, 0.0, float(E), ALU.is_lt, ALU.mult).then_inc(inv_n, 1)
            dve.wait_ge(inv_n, 1)
            dve.tensor_tensor(invf, invf, invn, ALU.add).then_inc(inv_w, 1)
            dve.wait_ge(inv_w, 1)
            dve.tensor_scalar(invf, invf, 0.0, float(E - 1), ALU.max, ALU.min).then_inc(inv_c, 1)
            dve.wait_ge(inv_c, 1)
            for n in (0, 1):
                last = dve.tensor_scalar(onehot[:, n * E:(n + 1) * E], invf, rowno[:, n:n + 1], None, ALU.is_equal)
            last.then_inc(onehot_ok, 1)
            dve.wait_ge(q_mm, 1)
            for m in range(KH):
                last = dve.tensor_scalar(q[:, m, :], PS[:, 2, m * BATCH:(m + 1) * BATCH], b3s[:, m:m + 1], 0.0,
                                         ALU.add, ALU.max)
            last.then_inc(q_ok, 1)

            def condition(c):
                xs = y[:, :, bass.ds(c * CH, CH)].rearrange("p k (b s) -> p k b s", s=SEQ)
                dve.wait_ge(x_in, c * 16 + 16)
                dve.wait_ge(xsum_ok, c)
                dve.tensor_reduce(vs.rearrange("p (k b) -> p k b", k=KH), xs, AX, ALU.add).then_inc(vsum_ok, 1)
                dve.wait_ge(vsum_ok, c + 1)
                dve.wait_ge(xc_hi, c)
                dve.wait_ge(xc_lo, c)
                for k in range(KH):
                    last = dve.scalar_tensor_tensor(
                        xc[:, k, :].rearrange("p (b s) -> p b s", s=SEQ), xs[:, k], float(SEQ),
                        vs[:, k * CB:(k + 1) * CB].unsqueeze(2).broadcast_to([P, CB, SEQ]), ALU.mult, ALU.add)
                last.then_inc(xsum_ok, 1)

            condition(0)
            dve.wait_ge(boot_hi, 1)
            dve.tensor_tensor(W2s[:, 1].rearrange("p k m -> p (k m)"), raw[:, BW2:BGW],
                              f32(W2s[:, 0].rearrange("p k m -> p (k m)")), sub).then_inc(w2_lo, 1)

            def shared_mul(c, b):
                n = SB[b][1]
                dve.wait_ge(s_sil, c * 3 + b + 1)
                dve.wait_ge(s_ahi, c * 3 + b)
                dve.wait_ge(s_alo, c * 3 + b)
                dve.tensor_tensor(mS[0:n, :], PS[0:n, 5, :], sS[0:n, :], ALU.mult).then_inc(s_mul, 1)

            def by_group(v):
                return v.rearrange("p j (f k) -> p (j f) k", k=K)

            def groups_masked(c):
                flat = PS[:, 3, TT * E:2 * TT * E].rearrange("p (j e) -> p j e", j=TT)
                dve.wait_ge(fl_mm, c + 1)
                dve.wait_ge(soft_ok, c)
                dve.tensor_scalar(z, flat, 0.0, NEG, ALU.is_equal, ALU.mult).then_inc(z_neg, 1)
                dve.wait_ge(sT_mm, c)
                dve.tensor_reduce(st[:, :, E:E + F], flat.rearrange("p j (f k) -> p j f k", k=K), AX, ALU.add
                                  ).then_inc(tot_ok, 1)
                dve.wait_ge(z_neg, c + 1)
                dve.tensor_tensor(z, z, flat, ALU.add).then_inc(z_all, 1)

            def groups_less_max(c):
                dve.wait_ge(z_all, c + 1)
                dve.tensor_reduce(gm, by_group(z), AX, ALU.max).then_inc(gm_ok, 1)
                dve.wait_ge(gm_ok, c + 1)
                dve.tensor_tensor(by_group(z), by_group(z), gm.unsqueeze(2).broadcast_to([P, TT * F, K]), sub
                                  ).then_inc(z_sub, 1)

            def groups_normalised(c):
                dve.wait_ge(z_exp, c + 1)
                dve.tensor_reduce(gs, by_group(z), AX, ALU.add).then_inc(gs_ok, 1)
                dve.wait_ge(gs_ok, c + 1)
                dve.reciprocal(gs, gs).then_inc(gr_ok, 1)
                dve.wait_ge(gr_ok, c + 1)
                dve.tensor_tensor(st[:, :, 0:E].rearrange("p j (f k) -> p j f k", k=K),
                                  z.rearrange("p j (f k) -> p j f k", k=K),
                                  gs.rearrange("p (j f) -> p j f", j=TT).unsqueeze(3).broadcast_to([P, TT, F, K]),
                                  ALU.mult).then_inc(soft_ok, 1)

            def shared_add(c):
                yc = y[:, :, bass.ds(c * CH, CH)]
                dve.wait_ge(sy_mm, c * 3 + 3)
                dve.tensor_tensor(yc, yc, pY, ALU.add).then_inc(sy_add, 1)

            def phase1(c, first, last):
                if not last:
                    condition(c + 1)
                if not first:
                    groups_masked(c - 1)
                shared_mul(c, 0)
                dve.wait_ge(tl_mm, c + 1)
                dve.wait_ge(dl_ok, c)
                dve.wait_ge(rep_ok, c)
                dve.tensor_reduce(lg, PS[:, 3, :].rearrange("p (j s e) -> p j e s", j=TT, s=2), AX, ALU.add
                                  ).then_inc(lg_ok, 1)
                dve.wait_ge(lg_ok, c + 1)
                if not first:
                    groups_less_max(c - 1)
                for j in range(TT):
                    mx = dve.max(top[:, j, :], lg[:, j, :])
                mx.then_inc(top_ok, 1)
                dve.wait_ge(top_ok, c + 1)
                dve.memset(top[:, :, TOPK:8], ABSENT).then_inc(absent_ok, 1)
                dve.wait_ge(absent_ok, c + 1)
                dve.wait_ge(ex_ok, c)
                dve.wait_ge(wsel_ok, c)
                dve.tensor_tensor(ex, lg, top[:, :, 0:1].broadcast_to([P, TT, E]), sub).then_inc(dl_ok, 1)
                for j in range(TT):
                    mr = dve.match_replace(rep[:, j, :], top[:, j, :], lg[:, j, :], GONE)
                mr.then_inc(rep_ok, 1)
                shared_mul(c, 1)
                if not first:
                    shared_add(c - 1)
                dve.wait_ge(ex_ok, c + 1)
                dve.tensor_reduce(sm, ex, AX, ALU.add).then_inc(sm_ok, 1)
                dve.wait_ge(sm_ok, c + 1)
                dve.reciprocal(rs, sm).then_inc(rs_ok, 1)
                dve.wait_ge(rep_ok, c + 1)
                dve.wait_ge(wT_mm, c)
                dve.scalar_tensor_tensor(wsel, rep, GONE / 2, ex, ALU.is_le, ALU.mult).then_inc(wsel_ok, 1)
                dve.wait_ge(wsel_ok, c + 1)
                dve.wait_ge(rs_ok, c + 1)
                dve.tensor_tensor(wsel, wsel, rs.unsqueeze(2).broadcast_to([P, TT, E]), ALU.mult).then_inc(wn_ok, 1)
                if not first:
                    groups_normalised(c - 1)
                shared_mul(c, 2)

            chunks(dve, phase1)
            groups_masked(NCH - 1)
            groups_less_max(NCH - 1)

            def g_rows(rows, e, out, cols, ok):
                dve.wait_ge(g_hi, e + 1)
                dve.scalar_tensor_tensor(out[rows, :], f32(Gh[rows, cols]), lomask[rows, :], pG[rows, cols],
                                         ALU.mult, ALU.add).then_inc(ok, 1)

            low, high = slice(0, 3 * K), slice(KR, KR + 3 * K)

            def g_adapters(e, wp):
                g_rows(APK, e, A3[:, wp, :], slice(XA, XA + P), a3_ok)

            def g_gate_up(e, wp):
                dve.wait_ge(piece_lo, e * PIECES + PIECES)
                g_rows(high, e, Wt[wp][:, 1, QGA:QGA + P + CW], slice(XGA, XGA + P + CW), g3g_ok)
                g_rows(low, e, Wt[wp][:, 1, QUB:QUB + P], slice(XUB, XUB + P), g3u_ok)

            def adapters_weighted(n):
                dve.wait_ge(a_mm[n.p], n.now)
                dve.wait_ge(wexp_in[n.p], n.same * 16 + 16)
                dve.wait_ge(vg_hi[1 - n.p], n.last)
                dve.wait_ge(vu_hi[1 - n.p], n.last)
                dve.wait_ge(xg_hi[1 - n.p], n.last)
                dve.wait_ge(xu_hi[1 - n.p], n.last)
                dve.wait_ge(vg_lo[1 - n.p], n.last)
                dve.wait_ge(vu_lo[1 - n.p], n.last)
                dve.tensor_tensor(ap, pa, wexp[n.p], ALU.mult).then_inc(ap_ok[n.p], 1)

            def adapters_low(n):
                g, u = slice(0, KR), slice(KR, P)
                dve.wait_ge(gB_mm[n.p], n.same)
                dve.wait_ge(vg_hi[n.p], n.now)
                dve.tensor_tensor(Vg[n.p][u, :], ap[g, :], f32(Vg[n.p][g, :]), sub).then_inc(vg_lo[n.p], 1)
                dve.wait_ge(vu_hi[n.p], n.now)
                dve.tensor_tensor(Vu[n.p][g, :], ap[u, :], f32(Vu[n.p][u, :]), sub).then_inc(vu_lo[n.p], 1)

            def add_y(n):
                yc = y[:, :, bass.ds(n.c * CH, CH)]
                dve.wait_ge(y_mm[n.p], n.now)
                dve.wait_ge(y_add[1 - n.p], n.last)
                dve.tensor_tensor(yc, yc, pY, ALU.add).then_inc(y_add[n.p], 1)

            g_adapters(0, 0)
            g_gate_up(0, 0)
            groups_normalised(NCH - 1)
            shared_add(NCH - 1)
            for prev, cur, nxt, (t, _j), more in steps(dve):
                if prev is None:
                    dve.wait_ge(wT_mm, NCH)
                    adapters_weighted(cur)
                    dve.wait_ge(sg_mm, 3 * NCH)
                    adapters_low(cur)
                with when(dve, t, (15, 16), more):
                    adapters_weighted(nxt)
                if prev is not None:
                    n = prev
                    dve.wait_ge(ad_cp[n.p], n.now)
                    dve.wait_ge(ad_hi[1 - n.p], n.last)
                    dve.wait_ge(ad_lo[1 - n.p], n.last)
                    dve.tensor_tensor(adp[0:KR, :], pad[0:KR, :], adc[0:KR, :], ALU.add).then_inc(ad_sum[n.p], 1)
                    dve.wait_ge(ad_sum[n.p], n.now)
                    dve.wait_ge(wdn_in[n.p], n.same * 16 + 16)
                    dve.tensor_tensor(adp[0:KR, :], adp[0:KR, :], wdn[n.p][0:KR, :], ALU.mult).then_inc(adp_ok[n.p], 1)
                    dve.wait_ge(ad_hi[n.p], n.now)
                    dve.tensor_tensor(Rlo[n.p][0:KR, :], adp[0:KR, :], f32(Rhi[n.p][0:KR, :]), sub
                                      ).then_inc(ad_lo[n.p], 1)
                with when(dve, t, (15, 16), more):
                    adapters_low(nxt)
                if prev is None:
                    dve.wait_ge(zeros_ok, 3)
                with when(dve, t, (16,), more):
                    n = cur
                    dve.wait_ge(scC[n.p], n.now)
                    dve.wait_ge(hiC[1 - n.p], n.last)
                    dve.wait_ge(loC[1 - n.p], n.last)
                    dve.tensor_tensor(mC[TAILS, :], pC[TAILS, :], sC[TAILS, :], ALU.mult).then_inc(mulC[n.p], 1)
                    dve.wait_ge(hiC[n.p], n.now)
                    dve.wait_ge(y_mm[n.p], n.same)
                    dve.tensor_tensor(Rlo[n.p][TAILS, :], mC[TAILS, :], f32(Rhi[n.p][TAILS, :]), sub
                                      ).then_inc(loC[n.p], 1)
                    dve.wait_ge(scA[n.p], n.now)
                    dve.wait_ge(gB_mm[n.p], n.now)
                    dve.wait_ge(hiA[1 - n.p], n.last)
                    dve.wait_ge(loA[1 - n.p], n.last)
                    dve.tensor_tensor(mA, pB, sA, ALU.mult).then_inc(mulA[n.p], 1)
                    dve.wait_ge(hiA[n.p], n.now)
                    dve.tensor_tensor(Alo[n.p], mA, f32(Ahi[n.p]), sub).then_inc(loA[n.p], 1)
                if prev is not None:
                    add_y(prev)
                if prev is None:
                    g_adapters(1, 1)
                if t in (8, 16):
                    with dve.If(more):
                        g_adapters(cur.e + 1, 1 - cur.w)
                if t == 7:
                    g_gate_up(cur.e + 1, 1)
                if t == 15:
                    with dve.If(more):
                        g_gate_up(cur.e + 1, 0)

        @block.gpsimd
        def _(pool):
            sub = ALU.subtract

            pool.wait_ge(boot_hi, 3)
            pool.tensor_tensor(GWs[:, :, E:2 * E], raw[:, BGW:BSG].rearrange("p (k m) -> p k m", k=KH),
                               f32(GWs[:, :, 0:E]), sub).then_inc(boot_lo, 1)

            def condition(c):
                for k in range(KH):
                    pool.wait_ge(q_ok, 1)
                    pool.wait_ge(xsum_ok, c + 1)
                    v = xc[:, k, :].rearrange("p (b s) -> p b s", s=SEQ)
                    qc = q[:, k, bass.ds(c * CB, CB)].unsqueeze(2).broadcast_to([P, CB, SEQ])
                    last = pool.tensor_tensor(v, v, qc, ALU.mult)
                last.then_inc(xc_ok, 1)
                pool.wait_ge(xc_hi, c + 1)
                pool.tensor_tensor(xcs[:, 1], xc, f32(xcs[:, 0]), sub).then_inc(xc_lo, 1)

            def h_low(c):
                pool.wait_ge(h_hi, c + 1)
                cols = bass.ds(c * CH, CH)
                pool.tensor_tensor(hs[:, 1, :, cols], hf, f32(hs[:, 0, :, cols]), sub).then_inc(h_lo, 1)

            def fold(e):
                pool.wait_ge(raw_in, e * 48 + 48)
                pool.tensor_tensor(raw[:, QB:QB + QW], raw[:, QB:QB + QW], scb[:, 0:QW], ALU.mult).then_inc(foldQ, 1)
                r = raw[0:KR, DN + H:DN + 2 * H]
                pool.tensor_tensor(r, r, scb[0:KR, QW:QW + H], ALU.mult).then_inc(foldR, 1)

            def piece(e, wp, z, before):
                cols = bass.ds(z * PW, PW)
                pool.wait_ge(foldQ, e + 1)
                pool.wait_ge(foldR, e + 1)
                if before is not None:
                    pool.wait_ge(y_mm[1], before)
                pool.tensor_copy(Wt[wp][:, 0, cols], raw[:, cols]).then_inc(piece_hi, 1)
                pool.wait_ge(piece_hi, e * PIECES + z + 1)
                pool.tensor_tensor(Wt[wp][:, 1, cols], raw[:, cols], f32(Wt[wp][:, 0, cols]), sub).then_inc(piece_lo, 1)

            def adapter_weights(e, wp):
                src = raw[:, ADR:MU].rearrange("p (k m) -> p k m", k=2)
                pool.tensor_copy(ADt[:, wp, :, 0:KR], src).then_inc(adw_hi, 1)
                pool.wait_ge(adw_hi, e + 1)
                pool.tensor_tensor(ADt[:, wp, :, KR:P], src, f32(ADt[:, wp, :, 0:KR]), sub).then_inc(adw_lo, 1)

            condition(0)
            pool.tensor_tensor(SGs[:, 1].rearrange("p k m -> p (k m)"), raw[:, BSG:BSD],
                               f32(SGs[:, 0].rearrange("p k m -> p (k m)")), sub).then_inc(boot_lo, 1)
            pool.wait_ge(boot_hi, 4)
            pool.tensor_tensor(SDs[:, 1].rearrange("p b m -> p (b m)"), SDraw,
                               f32(SDs[:, 0].rearrange("p b m -> p (b m)")), sub).then_inc(boot_lo, 1)
            h_low(0)

            def shared_low(c, b):
                n = SB[b][1]
                pool.wait_ge(s_ahi, c * 3 + b + 1)
                pool.tensor_tensor(hSs[0:n, b, 1, :], mS[0:n, :], f32(hSs[0:n, b, 0, :]), sub).then_inc(s_alo, 1)

            def group_rows_low(c):
                pool.wait_ge(s_hi, c + 1)
                pool.wait_ge(soft_out, c * 64)
                pool.tensor_tensor(sfs[0:E, 1, :], sTs[0:E, :], f32(sfs[0:E, 0, :]), sub).then_inc(s_lo, 1)

            def phase1(c, first, last):
                if not last:
                    condition(c + 1)
                shared_low(c, 0)
                if last:
                    adapter_weights(0, 0)
                elif not first:
                    piece(0, 0, c - 1, None)
                shared_low(c, 1)
                if not last:
                    h_low(c + 1)
                shared_low(c, 2)
                if first:
                    fold(0)
                else:
                    group_rows_low(c - 1)

            chunks(pool, phase1)
            for p in (0, 1):
                pool.memset(f32(Xu[p][0:KR, :]), 0.0).then_inc(zeros_ok, 1)
            group_rows_low(NCH - 1)
            pool.wait_ge(sy_add, NCH)
            pool.wait_ge(soft_out, 64 * NCH)
            pool.memset(sC, 0.0).then_inc(zeros_ok, 1)
            pool.wait_ge(zeros_ok, 3)
            for prev, cur, nxt, (t, j), more in steps(pool):
                with when(pool, t, (16,), more):
                    pool.wait_ge(scl_in[cur.p], cur.same * 16 + 16)
                    pool.wait_ge(silC[cur.p], cur.now)
                    pool.tensor_tensor(sC, sC, scl[cur.p], ALU.mult).then_inc(scC[cur.p], 1)
                    pool.wait_ge(silA[cur.p], cur.now)
                    pool.tensor_tensor(sA, sA, scl[cur.p], ALU.mult).then_inc(scA[cur.p], 1)
                if t == 0:
                    fold(1)
                if t in (8, 16):
                    with pool.If(more):
                        fold(cur.e + 1)
                if j is not None:
                    with when(pool, t, (9, 10), more):
                        piece(cur.e + 1, 1 - cur.w, j * 2 + (t - 1) % NCH, cur.e * (NCH // 2))
                if t == 7:
                    adapter_weights(cur.e + 1, 1)
                if t == 15:
                    with pool.If(more):
                        adapter_weights(cur.e + 1, 0)


def kernel(x, cond_1024, L0_cond_W3, L0_cond_b3, L0_cond_W2, L0_cond_b2, L0_ffn_gate_weight, L0_ffn_inv_mapping,
           L0_ffn_mask_up_W, L0_ffn_gate_W, L0_ffn_gate_qa, L0_ffn_gate_qb, L0_ffn_gate_scale, L0_ffn_up_W,
           L0_ffn_up_qa, L0_ffn_up_qb, L0_ffn_up_scale, L0_ffn_down_W, L0_ffn_down_qa, L0_ffn_down_qb,
           L0_ffn_down_scale, L0_ffn_sh_gate_W, L0_ffn_sh_up_W, L0_ffn_sh_down_W):
    import numpy as np
    import concourse.bacc as bacc
    from concourse.bass_utils import run_bass_kernel_spmd as run

    f = np.float32

    def tiles(a):
        return a.reshape(-1, P, a.shape[-1]).transpose(1, 0, 2)

    def T(a):
        return np.swapaxes(np.asarray(a), -1, -2)

    def rk(a):
        return np.asarray(a).transpose(0, 3, 1, 2).reshape(F, KR, a.shape[2])

    x = np.asarray(x)
    xT = tiles(T(x.reshape(TOKENS, H)))
    boot = np.zeros((P, BOOT), f)
    boot[:, BW2:BGW] = tiles(np.asarray(L0_cond_W2)).reshape(P, -1)
    boot[:, BGW:BSG] = tiles(T(L0_ffn_gate_weight)).reshape(P, -1)
    sgT, suT, sd = tiles(T(L0_ffn_sh_gate_W)), tiles(T(L0_ffn_sh_up_W)), T(L0_ffn_sh_down_W)
    boot[:, BSG:BSD] = np.concatenate([w[:, :, at:at + n] for at, n in SB for w in (sgT, suT)], axis=2).reshape(P, -1)
    for b, (at, n) in enumerate(SB):
        boot[0:n, BSD + b * H:BSD + (b + 1) * H] = sd[at:at + n]

    raw = np.zeros((F, P, RAWW), f)
    gW, uW = (T(w).reshape(F, KH, P, I) for w in (L0_ffn_gate_W, L0_ffn_up_W))
    qa = [rk(np.swapaxes(np.asarray(w), 2, 3)).transpose(0, 2, 1).reshape(F, KH, P, KR)
          for w in (L0_ffn_gate_qa, L0_ffn_up_qa)]
    mu = np.asarray(L0_ffn_mask_up_W).reshape(F, KH, P, K)
    for k in range(KH):
        o = k * XW
        raw[:, :, o + XA:o + XA + KR] = qa[0][:, k]
        raw[:, :, o + XA + KR:o + XA + P] = qa[1][:, k]
        raw[:, :, o + XGA:o + XGA + P] = gW[:, k, :, 0:P]
        raw[:, :, o + XC:o + XC + TAIL] = gW[:, k, :, P:I]
        raw[:, :, o + XC + KR:o + XC + CW] = uW[:, k, :, P:I]
        raw[:, :, o + XUB:o + XUB + P] = uW[:, k, :, 0:P]
        for row in (0, KR, P - 32):
            for part in range(3):
                at = MU + k * P + row + part * K
                raw[:, :, at:at + K] = mu[:, k]
    gq, uq = (rk(w) for w in (L0_ffn_gate_qb, L0_ffn_up_qb))
    scale = np.zeros((F, QW + H), f)
    gs, us = np.asarray(L0_ffn_gate_scale), np.asarray(L0_ffn_up_scale)
    for half in (0, KR):
        rows = slice(half, half + KR)
        raw[:, rows, QGA:QGA + P] = gq[:, :, 0:P]
        raw[:, rows, QGC:QGC + TAIL] = gq[:, :, P:I]
        raw[:, rows, QUB:QUB + P] = uq[:, :, 0:P]
        raw[:, rows, QUC + KR:QUC + CW] = uq[:, :, P:I]
    scale[:, QGA - QB:QGA - QB + P] = gs[:, 0:P]
    scale[:, QGC - QB:QGC - QB + TAIL] = gs[:, P:I]
    scale[:, QUB - QB:QUB - QB + P] = us[:, 0:P]
    scale[:, QUC - QB + KR:QUC - QB + CW] = us[:, P:I]
    scale[:, QW:] = np.asarray(L0_ffn_down_scale)
    dW = T(L0_ffn_down_W)
    raw[:, :, DN:DN + H] = dW[:, 0:P]
    raw[:, 0:KR, DN + H:DN + 2 * H] = rk(L0_ffn_down_qb)
    raw[:, KR:CW, DN + H:DN + 2 * H] = dW[:, P:I]
    da = rk(np.swapaxes(np.asarray(L0_ffn_down_qa), 2, 3)).transpose(0, 2, 1)
    raw[:, :, ADR:ADR + KR] = da[:, 0:P]
    raw[:, KR:CW, ADR + KR:ADR + 2 * KR] = da[:, P:I]

    consts = np.zeros((P, CONSTS), f)
    consts[:, 0:P] = np.eye(P)
    for row in (0, KR, P - 32):
        consts[row + 2 * K:row + 3 * K, P] = -1.0
    consts[:, P + 1] = np.arange(P)
    consts[:, P + 2] = np.arange(P) - E
    vecs = np.concatenate([np.asarray(v).reshape(KH, P).T for v in (L0_cond_b3, L0_cond_b2)], axis=1)

    arrays = {
        "xT": xT, "condT": T(cond_1024), "W3": np.asarray(L0_cond_W3), "vecs": vecs, "consts": consts,
        "inv": np.asarray(L0_ffn_inv_mapping), "boot": boot, "raw": raw.reshape(F * P, RAWW), "scale": scale,
    }
    arrays = {"in_" + n: np.ascontiguousarray(a) for n, a in arrays.items()}
    nc = bacc.Bacc("TRN2", target_bir_lowering=False, num_devices=1)
    args = [nc.dram_tensor(n, a.shape, mybir.dt.from_np(a.dtype), kind="ExternalInput").ap() for n, a in arrays.items()]
    out = nc.dram_tensor("out_T", (P, KH, TOKENS), F32, kind="ExternalOutput").ap()
    build(nc, *args, out)
    got = run(nc, [arrays], core_ids=[0]).results[0]["out_T"]
    return got.transpose(2, 1, 0).reshape(BATCH, SEQ, H)
```

```python
from contextlib import ExitStack, nullcontext

import concourse.bass as bass
from concourse import mybir

F32 = mybir.dt.float32
F32R = mybir.dt.float32r
I32 = mybir.dt.int32
ALU = mybir.AluOpType
ACT = mybir.ActivationFunctionType
AX = mybir.AxisListType.X

P = 128
BATCH, SEQ, H, COND = 128, 32, 256, 128
TOKENS = BATCH * SEQ
CH = 512
NCH = TOKENS // CH
CB = CH // SEQ
TT = CH // P
KH = H // P
E, F, K, R, TOPK = 64, 8, 8, 8, 6
KR = K * R
I = 176
TAIL = I - P
CW = KR + TAIL
ISH = 2 * I
SB = [(0, ISH - 2 * P), (ISH - 2 * P, P), (ISH - P, P)]
ROUTER = slice(P - E // 2, P)
assert SB[0][1] == ROUTER.start

XA, XGA, XC, XUB, XW = 0, P, 2 * P, 2 * P + CW, 3 * P + CW
QB = KH * XW
QGA, QGC, QUC, QUB = QB, QB + P, QB + P + CW, QB + P + 2 * CW
QW = 2 * P + 2 * CW
DN = QB + QW
SPLIT = DN + 2 * H
PIECES = NCH - 2
PW = -(-SPLIT // (2 * PIECES)) * 2
SPLITW = PW * PIECES
ADR = SPLITW
MU = ADR + 2 * KR
RAWW = MU + KH * P
SGW = 3 * 2 * P
BW2, BSG, BSD = 0, KH * H, KH * H + KH * SGW
BOOT = BSD + 3 * H
CONSTS = P + 3
NEG = -1.0e9
GONE = -3.0e38
ABSENT = 3.0e38


class Unit:

    def __init__(self, e, c, k, p, w):
        self.e, self.c, self.k, self.p, self.w = e, c, k, p, w
        self.now, self.last, self.same = k + 1, k + p, k


def steps(eng):
    def unit(i, t, j=0):
        return Unit(i * 2 + t // NCH, j * 2 + t % NCH, i * NCH + (j + t // 2), t % 2, (t // NCH) % 2)

    yield None, unit(0, 0), unit(0, 1), (0, None), None
    pairs = F // 2
    with eng.Fori(0, pairs) as i:
        for t0 in (0, NCH):
            with eng.Fori(0, (NCH - 2) // 2) as j:
                for t in (t0 + 1, t0 + 2):
                    yield unit(i, t - 1, j), unit(i, t, j), unit(i, t + 1, j), (t, j), i < pairs - 1
            for t in (t0 + NCH - 1, t0 + NCH):
                yield unit(i, t - 1), unit(i, t), unit(i, t + 1), (t, None), i < pairs - 1


def build(nc, xT, condT, W3, vecs, consts, inv, boot, raw_d, scale_d, outT):
    soft_d = nc.dram_tensor("soft_scratch", (NCH * (E + F), CH), F32, kind="Internal").ap()
    packed_d = nc.dram_tensor("packed_scratch", (NCH * 3 * E, CH), F32, kind="Internal").ap()

    with ExitStack() as ctx:
        def sb(name, cols, dt=F32):
            return ctx.enter_context(nc.sbuf_tensor(name, [P, cols], dt))

        def carve(arena, sizes):
            out, at = [], 0
            for n in sizes:
                out.append(arena[:, at:at + n])
                at += n
            assert at <= arena.shape[1], (at, arena.shape)
            return out

        y = sb("y", KH * TOKENS)[:, :].rearrange("p (k t) -> p k t", k=KH)
        hs = sb("h_split", 2 * KH * TOKENS, F32R)[:, :].rearrange("p (s k t) -> p s k t", s=2, k=KH)
        W_even = sb("W_even", 2 * SPLITW, F32R)
        ADt = sb("down_adapter", 2 * 2 * P, F32R)[:, :].rearrange("p (w k m) -> p w k m", w=2, k=2)
        A3 = sb("a_packed", 2 * P, F32R)[:, :].rearrange("p (w m) -> p w m", w=2)
        Gh = sb("G_hi", XW, F32R)
        raw = sb("raw", RAWW)
        scb = sb("scales", QW + H)
        q = sb("q_emb", KH * BATCH)[:, :].rearrange("p (k b) -> p k b", k=KH)
        cst = sb("consts", CONSTS)
        eye, lomask, rowno = cst[:, 0:P], cst[:, P:P + 1], cst[:, P + 1:P + 3]
        onehot = sb("onehot", 2 * E)
        vec = sb("vectors", 2 * KH)
        seed = sb("table_seed", 2)
        b3s, b2s = vec[:, 0:KH], vec[:, KH:2 * KH]

        tail2 = sb("tail_hi_lo", CH, F32R)
        RA = sb("arena_r", 16 * CH + 2 * SPLITW, F32R)
        FA = sb("arena_f", 13 * CH)
        used = 2 * KH * CH + CH + 5 * TT * E + TT * (E + F) + TT * E + 2 * CH + TT * 8 + 2 * TT + 2 * TT * F + KH * CB
        LEFT = 13 * CH - used - CH

        (W2s, SGs, SDs, xcs, hSs, sfs) = carve(
            RA, [2 * KH * H, 2 * KH * SGW, 2 * 3 * H, 2 * KH * CH, 3 * 2 * CH, 2 * CH])
        W2s = W2s.rearrange("p (s k m) -> p s k m", s=2, k=KH)
        SGs = SGs.rearrange("p (s k m) -> p s k m", s=2, k=KH)
        SDs = SDs.rearrange("p (s b m) -> p s b m", s=2, b=3)
        xcs = xcs.rearrange("p (s k t) -> p s k t", s=2, k=KH)
        hSs = hSs.rearrange("p (b s t) -> p b s t", b=3, s=2)
        sfs = sfs.rearrange("p (s t) -> p s t", s=2)
        (xc_, hf_, RLs, lg, ex, rep, wsel, z, st, wTs, sS, mS, top, sm, rs, gm, gs, vs, _, sTs) = carve(
            FA, [KH * CH, KH * CH, CH, TT * E, TT * E, TT * E, TT * E, TT * E, TT * (E + F), TT * E, CH, CH,
                 TT * 8, TT, TT, TT * F, TT * F, KH * CB, LEFT, CH])
        xc = xc_.rearrange("p (k t) -> p k t", k=KH)
        hf = hf_.rearrange("p (k t) -> p k t", k=KH)
        lg, ex, rep, wsel, z, st, top = (v.rearrange("p (j e) -> p j e", j=TT)
                                         for v in (lg, ex, rep, wsel, z, st, top))
        W3s, cTs, invs = sS[:, 0:H], sS[:, H:H + BATCH], z[:, 0, :].bitcast(I32)
        invf, invn = ex[:, 0, :], ex[:, 1, :]
        SDraw = FA[:, used:used + 3 * H]

        r2 = carve(RA, [CH] * 16 + [2 * SPLITW])
        Vg, Vu, Xg, Xu, Ahi, Alo, Rhi, Rlo = (r2[2 * n:2 * n + 2] for n in range(8))
        Wt = [W_even[:, :].rearrange("p (s m) -> p s m", s=2), r2[16].rearrange("p (s m) -> p s m", s=2)]
        f2 = carve(FA, [CH] * 13)
        wexp, wdn, scl = (f2[2 * n:2 * n + 2] for n in range(3))
        ap, sA, sC, mA, mC, adc, adp = f2[6:13]

        PS = ctx.enter_context(nc.psum_tensor("ps", [P, 8, CH], F32))
        pC, pA, pB, pG, pad, pa = (PS[:, n, :] for n in range(6))
        pY = PS[:, 6:8, :]
        APK = slice(P - 32, P - 32 + 3 * K)
        TAILS = slice(KR, CW)

        def sem(name):
            return ctx.enter_context(nc.semaphore(name))

        def sems(names):
            return [sem(n) for n in names.split()]

        def pairs(names):
            return [[sem(n + "_even"), sem(n + "_odd")] for n in names.split()]

        (q_in, consts_in, x_in, w2_in, sg_in, sd_in, raw_in, soft_out, y_out) = sems(
            "q_in consts_in x_in w2_in sg_in sd_in raw_in soft_out y_out")
        (inv_f, inv_n, inv_w, inv_c, onehot_ok, q_mm, q_ok) = sems("inv_f inv_n inv_w inv_c onehot_ok q_mm q_ok")
        (seed_ok, boot_hi, w2_lo, boot_lo, xc_hi0, hf0_ok, h_hi0) = sems(
            "seed_ok boot_hi w2_lo boot_lo xc_hi0 hf0_ok h_hi0")
        (vsum_ok, xsum_ok, xc0_ok, xc_ok, xc_hi, xc_lo, h_mm, hf_ok, h_hi, h_lo, rl_zero, rl_cp, tl_mm, lg_ok) = sems(
            "vsum_ok xsum_ok xc0_ok xc_ok xc_hi xc_lo h_mm hf_ok h_hi h_lo rl_zero rl_cp tl_mm lg_ok")
        (top_ok, absent_ok, rep_ok, dl_ok, ex_ok, sm_ok, rs_ok, wsel_ok, wn_ok, wT_mm, wT_cp, fl_mm) = sems(
            "top_ok absent_ok rep_ok dl_ok ex_ok sm_ok rs_ok wsel_ok wn_ok wT_mm wT_cp fl_mm")
        (z_neg, z_all, tot_ok, gm_ok, z_sub, z_exp, gs_ok, gr_ok, soft_ok, sT_mm, sT_cp, s_hi, s_lo) = sems(
            "z_neg z_all tot_ok gm_ok z_sub z_exp gs_ok gr_ok soft_ok sT_mm sT_cp s_hi s_lo")
        (sg_mm, s_sil, s_mul, s_ahi, s_alo, sy_mm, sy_add) = sems("sg_mm s_sil s_mul s_ahi s_alo sy_mm sy_add")
        a_mm, gA_mm, gB_mm, gC_mm, ad_mm, y_mm = pairs("a_mm gA_mm gB_mm gC_mm ad_mm y_mm")
        ap_ok, vg_lo, vu_lo, ad_sum, adp_ok, ad_lo, mulA, loA, mulC, loC, y_add = pairs(
            "ap_ok vg_lo vu_lo ad_sum adp_ok ad_lo mulA loA mulC loC y_add")
        vg_hi, vu_hi, xg_hi, xu_hi, ad_cp, silA, ad_hi, hiA, silC, hiC, thiC, tloC = pairs(
            "vg_hi vu_hi xg_hi xu_hi ad_cp silA ad_hi hiA silC hiC thiC tloC")
        scA, scC, wexp_in, wdn_in, scl_in, pk_in, pka_in = pairs("scA scC wexp_in wdn_in scl_in pk_in pka_in")
        (foldQ, foldR, piece_hi, piece_lo, adw_hi, adw_lo, g_mm, g_hi, a3_ok, g3g_ok, g3u_ok, zeros_ok) = sems(
            "foldQ foldR piece_hi piece_lo adw_hi adw_lo g_mm g_hi a3_ok g3g_ok g3u_ok zeros_ok")

        def f32(v):
            return v.bitcast(F32)

        def when(eng, t, steps_, cond):
            return eng.If(cond) if t in steps_ else nullcontext()

        def real(e):
            if isinstance(e, int):
                return e
            return nc.s_assert_within(e, 0, F - 1, skip_runtime_bounds_check_because="left out in the last pair")

        def chunks(eng, body):
            body(0, True, False)
            with eng.Fori(1, NCH - 1) as c:
                body(c, False, False)
            body(NCH - 1, False, True)

        block = ctx.enter_context(nc.Block())

        @block.sync
        def _(sp):
            sp.dma_start(y[:, :, 0:CH], xT[:, :, 0:CH]).then_inc(x_in, 16)
            sp.dma_start(W3s, W3).then_inc(q_in, 16)
            sp.dma_start(raw[:, BW2:BSG], boot[:, BW2:BSG]).then_inc(w2_in, 16)
            sp.dma_start(raw[:, BSG:BSD], boot[:, BSG:BSD]).then_inc(sg_in, 16)
            sp.dma_start(SDraw, boot[:, BSD:BOOT]).then_inc(sd_in, 16)

            def load_x(c):
                sp.wait_ge(x_in, c * 16)
                sp.dma_start(y[:, :, bass.ds(c * CH, CH)], xT[:, :, bass.ds(c * CH, CH)]).then_inc(x_in, 16)

            load_x(1)
            load_x(2)

            def load_split(e):
                e = real(e)
                sp.dma_start(raw[:, 0:SPLITW], raw_d[bass.ds(e * P, P), 0:SPLITW]).then_inc(raw_in, 16)

            def load_rest(e):
                e = real(e)
                sp.dma_start(raw[:, ADR:RAWW], raw_d[bass.ds(e * P, P), ADR:RAWW]).then_inc(raw_in, 16)
                row = scale_d[bass.ds(e, 1), :]
                sp.dma_start(scb[:, :], bass.AP(row.tensor, row.offset, [[0, P], [1, QW + H]])).then_inc(raw_in, 16)

            sp.wait_ge(boot_hi, 3)
            sp.wait_ge(w2_lo, 1)
            sp.wait_ge(boot_lo, 2)
            load_split(0)
            load_rest(0)
            with sp.Fori(3, NCH) as c:
                load_x(c)

            def store(c):
                sp.wait_ge(sT_cp, c + 1)
                sp.dma_start(soft_d[bass.ds(c * (E + F), E + F), :], sTs[0:E + F, :]).then_inc(soft_out, 16)
                sp.wait_ge(s_hi, c + 1)
                sp.dma_start(packed_d[bass.ds(c * 3 * E, E), :], f32(sfs[0:E, 0, :])).then_inc(soft_out, 16)
                sp.dma_start(packed_d[bass.ds(c * 3 * E + 2 * E, E), :], f32(sfs[0:E, 0, :])).then_inc(soft_out, 16)
                sp.wait_ge(s_lo, c + 1)
                sp.dma_start(packed_d[bass.ds(c * 3 * E + E, E), :], f32(sfs[0:E, 1, :])).then_inc(soft_out, 16)

            def next_split(e):
                sp.wait_ge(piece_hi, e * PIECES)
                sp.wait_ge(piece_lo, e * PIECES)
                sp.wait_ge(g_mm, e)
                load_split(e)

            def next_rest(e):
                sp.wait_ge(adw_hi, e)
                sp.wait_ge(adw_lo, e)
                load_rest(e)

            with sp.Fori(0, NCH - 2) as c:
                store(c)
            next_split(1)
            next_rest(1)

            def load_unit(n):
                e = real(n.e)
                row = soft_d[bass.ds(n.c * (E + F) + e * K, K), :]
                part = packed_d[bass.ds(n.c * 3 * E + e * K, K), :]
                total = soft_d[bass.ds(n.c * (E + F) + e + E, 1), :]
                packed = bass.AP(part.tensor, part.offset, [[E * CH, 3], [CH, K], [1, CH]])
                sp.wait_ge(a_mm[n.p], n.same)
                sp.dma_start(f32(Xg[n.p][APK, :]), packed).then_inc(pka_in[n.p], 16)
                sp.wait_ge(ap_ok[n.p], n.same)
                sp.dma_start(wexp[n.p], bass.AP(row.tensor, row.offset, [[0, 2 * R], [CH, K], [1, CH]])
                             ).then_inc(wexp_in[n.p], 16)
                sp.wait_ge(gB_mm[n.p], n.same)
                sp.dma_start(f32(Xu[n.p][0:3 * K, :]), packed).then_inc(pk_in[n.p], 16)
                sp.dma_start(f32(Xg[n.p][KR:KR + 3 * K, :]), packed).then_inc(pk_in[n.p], 16)
                sp.wait_ge(scA[n.p], n.same)
                sp.wait_ge(scC[n.p], n.same)
                sp.dma_start(scl[n.p], bass.AP(total.tensor, total.offset, [[0, P], [1, CH]])
                             ).then_inc(scl_in[n.p], 16)
                sp.wait_ge(adp_ok[n.p], n.same)
                sp.dma_start(wdn[n.p][0:KR, :], bass.AP(row.tensor, row.offset, [[0, R], [CH, K], [1, CH]])
                             ).then_inc(wdn_in[n.p], 16)

            for prev, cur, nxt, (t, _j), more in steps(sp):
                if prev is None:
                    sp.wait_ge(soft_out, 64 * (NCH - 2))
                    sp.wait_ge(sg_mm, 3 * NCH)
                    sp.wait_ge(wn_ok, NCH)
                    sp.wait_ge(zeros_ok, 2)
                    load_unit(cur)
                    load_unit(nxt)
                    store(NCH - 2)
                    store(NCH - 1)
                    continue
                with when(sp, t, (15, 16), more):
                    load_unit(nxt)
                if t == 2:
                    sp.wait_ge(soft_out, 64 * NCH)
                if t in (7, 15):
                    with sp.If(more):
                        next_split(cur.e + 2)
                if t in (8, 16):
                    with sp.If(more):
                        next_rest(cur.e + 1)
            with sp.Fori(0, NCH // 2) as c:
                for p in (0, 1):
                    sp.wait_ge(y_add[p], c + ((F - 1) * NCH // 2 + 1))
                    sp.dma_start(outT[:, :, bass.ds((c * 2 + p) * CH, CH)], y[:, :, bass.ds((c * 2 + p) * CH, CH)]
                                 ).then_inc(y_out, 16)
            sp.wait_ge(y_out, 16 * NCH)

        @block.tensor
        def _(pe):
            def product(out, parts, first=True, last=True):
                for n, (lhsT, rhs) in enumerate(parts):
                    mm = pe.matmul(out, lhsT, rhs, start=first and n == 0, stop=last and n == len(parts) - 1)
                return mm

            def three(w_hi, w_lo, v_hi, v_lo):
                return [(w_hi, v_hi), (w_lo, v_hi), (w_hi, v_lo)]

            pe.wait_ge(q_in, 16 * 3)
            for m in range(KH):
                mm = product(PS[:, 2, m * BATCH:(m + 1) * BATCH], [(W3s[:, m * P:(m + 1) * P], cTs)])
            mm.then_inc(q_mm, 1)

            def h_products(c):
                pe.wait_ge(xc_hi, c + 1)
                pe.wait_ge(xc_lo, c + 1)
                pe.wait_ge(hf_ok, c)
                for m in range(KH):
                    ms = slice(m * P, (m + 1) * P)
                    parts = [x for k in range(KH) for x in
                             three(W2s[:, 0, k, ms], W2s[:, 1, k, ms], xcs[:, 0, k, :], xcs[:, 1, k, :])]
                    product(PS[:, m, :], parts).then_inc(h_mm, 1)

            def h_of(c):
                return [[hs[:, s, k, bass.ds(c * CH, CH)] for k in range(KH)] for s in (0, 1)]

            pe.wait_ge(boot_hi, 1)
            pe.wait_ge(w2_lo, 1)
            h_products(0)
            pe.wait_ge(consts_in, 16 * 2)
            pe.wait_ge(onehot_ok, 1)
            pe.wait_ge(boot_hi, 3)
            pe.wait_ge(boot_lo, 2)

            def shared_up(c, b):
                hh, hl = h_of(c)
                pe.wait_ge(s_mul, c * 3 + b)
                if b == 1:
                    pe.wait_ge(rl_cp, c + 1)
                for g in (0, 1):
                    ms = slice((2 * b + g) * P, (2 * b + g + 1) * P)
                    mm = product(PS[:, 4 + g, :], [x for k in range(KH) for x in
                                                     three(SGs[:, 0, k, ms], SGs[:, 1, k, ms], hh[k], hl[k])])
                mm.then_inc(sg_mm, 1)

            def shared_down(c, b):
                n = SB[b][1]
                pe.wait_ge(s_ahi, c * 3 + b + 1)
                pe.wait_ge(s_alo, c * 3 + b + 1)
                if b == 0:
                    pe.wait_ge(sy_add, c)
                for m in range(KH):
                    ms = slice(m * P, (m + 1) * P)
                    mm = product(PS[:, 6 + m, :], three(SDs[0:n, 0, b, ms], SDs[0:n, 1, b, ms],
                                                        hSs[0:n, b, 0, :], hSs[0:n, b, 1, :]),
                                 first=b == 0, last=b == 2)
                mm.then_inc(sy_mm, 1)

            def gather(c):
                pe.wait_ge(wT_cp, c + 1)
                for j in range(TT // 2):
                    mm = product(PS[:, 3, (TT // 2 + j) * P:(TT // 2 + j + 1) * P],
                                 [(wTs[:, j * P:(j + 1) * P], onehot[:, :])])
                mm.then_inc(fl_mm, 1)

            def groups_to_rows(c):
                pe.wait_ge(soft_ok, c + 1)
                pe.wait_ge(tot_ok, c + 1)
                pe.wait_ge(sT_cp, c)
                for j in range(TT):
                    mm = pe.transpose(PS[0:E + F, 2, j * P:(j + 1) * P], st[:, j, :], eye)
                mm.then_inc(sT_mm, 1)

            def g_products(e, bank):
                pe.wait_ge(raw_in, e * 48 + 48)
                pe.wait_ge(a3_ok, e)
                pe.wait_ge(g3g_ok, e)
                pe.wait_ge(g3u_ok, e)
                product(bank[:, 0:XW], [(raw[:, MU + k * P:MU + (k + 1) * P], raw[:, k * XW:(k + 1) * XW])
                                        for k in range(KH)]).then_inc(g_mm, 1)

            def phase1(c, first, last):
                pe.wait_ge(h_hi, c + 1)
                pe.wait_ge(h_lo, c + 1)
                shared_up(c, 0)
                if not first:
                    gather(c - 1)
                    shared_down(c - 1, 2)
                pe.wait_ge(rl_cp, c + 1)
                pe.wait_ge(tot_ok, c)
                pe.wait_ge(z_all, c)
                for j in range(TT):
                    mm = pe.transpose(PS[:, 3, j * P:(j + 1) * P], RLs[:, j * P:(j + 1) * P], eye)
                mm.then_inc(tl_mm, 1)
                shared_up(c, 1)
                if last:
                    pe.wait_ge(hf_ok, NCH)
                    g_products(0, pA)
                else:
                    h_products(c + 1)
                shared_up(c, 2)
                shared_down(c, 0)
                if not first and not last:
                    groups_to_rows(c - 1)
                shared_down(c, 1)
                if last:
                    groups_to_rows(c - 1)
                pe.wait_ge(wn_ok, c + 1)
                pe.wait_ge(lg_ok, c + 1)
                for j in range(TT // 2):
                    mm = pe.transpose(PS[:, 3, j * P:(j + 1) * P], wsel[:, 2 * j:2 * j + 2, :], eye)
                mm.then_inc(wT_mm, 1)

            chunks(pe, phase1)

            def w(n, s, at, width=P, rows=slice(0, P)):
                return Wt[n.w][rows, s, at:at + width]

            def from_h(n, at, width=P):
                hh, hl = h_of(n.c)
                return [x for k in range(KH) for x in
                        three(w(n, 0, k * XW + at, width), w(n, 1, k * XW + at, width), hh[k], hl[k])]

            def adapters_in(n, fresh):
                if fresh:
                    pe.wait_ge(piece_hi, n.e * PIECES + PIECES)
                    pe.wait_ge(piece_lo, n.e * PIECES + PIECES)
                    pe.wait_ge(a3_ok, n.e + 1)
                pe.wait_ge(ap_ok[1 - n.p], n.last)
                product(pa, from_h(n, XA), last=False)
                pe.wait_ge(pka_in[n.p], n.same * 16 + 16)
                product(pa, [(A3[APK, n.w, :], Xg[n.p][APK, :])], first=False).then_inc(a_mm[n.p], 1)

            def down_adapter(n, fresh):
                if fresh:
                    pe.wait_ge(adw_hi, n.e + 1)
                    pe.wait_ge(adw_lo, n.e + 1)
                pe.wait_ge(hiA[n.p], n.now)
                pe.wait_ge(loA[n.p], n.now)
                pe.wait_ge(thiC[n.p], n.now)
                pe.wait_ge(tloC[n.p], n.now)
                pe.wait_ge(ad_sum[1 - n.p], n.last)
                product(pad, [(ADt[0:CW, n.w, 1, :], tail2[0:CW, :]),
                              (ADt[:, n.w, 0, :], Ahi[n.p]), (ADt[:, n.w, 0, :], Alo[n.p])]).then_inc(ad_mm[n.p], 1)

            def gate_up(n, fresh, starting=False):
                packed = slice(0, KR + 3 * K)
                if fresh:
                    pe.wait_ge(g3g_ok, n.e + 1)
                    pe.wait_ge(g3u_ok, n.e + 1)
                pe.wait_ge(mulC[1 - n.p], n.last)
                product(pC[0:CW, :], from_h(n, XC, CW), last=False)
                pe.wait_ge(vg_hi[n.p], n.now)
                pe.wait_ge(vg_lo[n.p], n.now)
                pe.wait_ge(xg_hi[n.p], n.now)
                pe.wait_ge(vu_hi[n.p], n.now)
                pe.wait_ge(vu_lo[n.p], n.now)
                pe.wait_ge(xu_hi[n.p], n.now)
                pe.wait_ge(pk_in[n.p], n.same * 32 + 32)
                up = slice(KR, P)
                product(pC[0:CW, :], [
                    (w(n, 0, QGC, CW), Vg[n.p]), (w(n, 1, QGC, CW, packed), Xg[n.p][packed, :]),
                    (w(n, 0, QUC, CW), Vu[n.p]), (w(n, 1, QUC, CW, up), Xu[n.p][up, :])],
                    first=False).then_inc(gC_mm[n.p], 1)
                if starting:
                    groups_to_rows(NCH - 1)
                pe.wait_ge(silA[1 - n.p], n.last)
                product(pA, from_h(n, XGA) + [(w(n, 0, QGA), Vg[n.p]), (w(n, 1, QGA, P, packed), Xg[n.p][packed, :])]
                        ).then_inc(gA_mm[n.p], 1)
                if starting:
                    pe.wait_ge(sT_cp, NCH)
                pe.wait_ge(mulA[1 - n.p], n.last)
                product(pB, from_h(n, XUB) + [(w(n, 0, QUB), Vu[n.p]), (w(n, 1, QUB), Xu[n.p])]
                        ).then_inc(gB_mm[n.p], 1)

            def down(n):
                pe.wait_ge(y_add[1 - n.p], n.last)
                for m in range(KH):
                    dA = DN + m * P
                    product(pY[:, m, :], three(w(n, 0, dA), w(n, 1, dA), Ahi[n.p], Alo[n.p]), last=False)
                pe.wait_ge(hiC[n.p], n.now)
                pe.wait_ge(loC[n.p], n.now)
                pe.wait_ge(ad_hi[n.p], n.now)
                pe.wait_ge(ad_lo[n.p], n.now)
                r = slice(0, CW)
                for m in range(KH):
                    dR = DN + H + m * P
                    parts = three(w(n, 0, dR, P, r), w(n, 1, dR, P, r), Rhi[n.p][r, :], Rlo[n.p][r, :])
                    mm = product(pY[:, m, :], parts, first=False)
                mm.then_inc(y_mm[n.p], 1)

            for prev, cur, nxt, (t, _j), more in steps(pe):
                if prev is None:
                    pe.wait_ge(s_mul, 3 * NCH)
                    adapters_in(cur, True)
                    gather(NCH - 1)
                    shared_down(NCH - 1, 2)
                    adapters_in(nxt, False)
                    gate_up(cur, True, starting=True)
                    pe.wait_ge(z_all, NCH)
                    pe.wait_ge(tot_ok, NCH)
                    g_products(1, pG)
                    continue
                with when(pe, t, (15, 16), more):
                    adapters_in(nxt, t in (7, 15))
                down_adapter(prev, t in (1, 9))
                with when(pe, t, (16,), more):
                    gate_up(cur, t in (8, 16))
                down(prev)
                if t in (8, 16):
                    with pe.If(more):
                        g_products(cur.e + 1, pG)

        @block.scalar
        def _(act):
            def copy(out, in_):
                return act.activation(out, in_, ACT.Copy)

            def load_silu():
                act.wait_ge(seed_ok, 1)
                act.activation(seed[:, 1:2], seed[:, 0:1], ACT.Silu)

            act.dma_start(cTs, condT).then_inc(q_in, 16)
            act.dma_start(vec[:, :], vecs).then_inc(q_in, 16)
            act.dma_start(cst[:, :], consts).then_inc(consts_in, 16)
            act.dma_start(invs, bass.AP(inv.tensor, 0, [[0, P], [1, E]])).then_inc(consts_in, 16)

            load_silu()
            act.wait_ge(q_in, 16 * 3)
            act.wait_ge(q_mm, 1)
            for m in range(KH):
                last = act.activation(q[:, m, :], PS[:, 2, m * BATCH:(m + 1) * BATCH], ACT.Relu, bias=b3s[:, m:m + 1])
            last.then_inc(q_ok, 1)
            act.wait_ge(w2_in, 16)
            copy(W2s[:, 0].rearrange("p k m -> p (k m)"), raw[:, BW2:BSG]).then_inc(boot_hi, 1)

            def condition_high(c):
                act.wait_ge(xc0_ok, c + 1)
                act.wait_ge(xc_ok, c + 1)
                act.wait_ge(h_mm, c * KH)
                copy(xcs[:, 0], xc).then_inc(xc_hi, 1)

            def h_high(c):
                act.wait_ge(h_hi, c)
                act.wait_ge(h_lo, c)
                for m in range(KH):
                    act.wait_ge(h_mm, c * KH + m + 1)
                    last = act.activation(hf[:, m, :], PS[:, m, :], ACT.Relu, bias=b2s[:, m:m + 1])
                last.then_inc(hf_ok, 1)
                act.wait_ge(hf_ok, c + 1)
                copy(hs[:, 0, :, bass.ds(c * CH, CH)], hf).then_inc(h_hi, 1)

            act.wait_ge(xc0_ok, 1)
            copy(xcs[:, 0, 0], xc[:, 0]).then_inc(xc_hi0, 1)
            act.wait_ge(xc_ok, 1)
            copy(xcs[:, 0, 1], xc[:, 1]).then_inc(xc_hi, 1)
            act.wait_ge(sg_in, 16)
            copy(SGs[:, 0].rearrange("p k m -> p (k m)"), raw[:, BSG:BSD]).then_inc(boot_hi, 1)
            act.wait_ge(sd_in, 16)
            copy(SDs[:, 0].rearrange("p b m -> p (b m)"), SDraw).then_inc(boot_hi, 1)
            for m in range(KH):
                act.wait_ge(h_mm, m + 1)
                act.activation(hf[:, m, :], PS[:, m, :], ACT.Relu, bias=b2s[:, m:m + 1]
                               ).then_inc((hf0_ok, hf_ok)[m], 1)
                act.wait_ge((hf0_ok, hf_ok)[m], 1)
                copy(hs[:, 0, m, 0:CH], hf[:, m, :]).then_inc((h_hi0, h_hi)[m], 1)
            act.wait_ge(boot_hi, 3)
            act.wait_ge(boot_lo, 2)

            def shared_silu(c, b):
                n = SB[b][1]
                act.wait_ge(sg_mm, c * 3 + b + 1)
                act.wait_ge(s_mul, c * 3 + b)
                act.activation(sS[0:n, :], PS[0:n, 4, :], ACT.Silu).then_inc(s_sil, 1)

            def shared_high(c, b, first):
                n = SB[b][1]
                act.wait_ge(s_mul, c * 3 + b + 1)
                if not first:
                    act.wait_ge(sy_mm, c * 3 + b - 2)
                copy(hSs[0:n, b, 0, :], mS[0:n, :]).then_inc(s_ahi, 1)

            def routed_rows(c):
                act.wait_ge(wT_mm, c + 1)
                act.wait_ge(fl_mm, c)
                copy(wTs, PS[:, 3, 0:TT * E]).then_inc(wT_cp, 1)

            def groups_exp(c):
                act.wait_ge(z_sub, c + 1)
                act.activation(z, z, ACT.Exp).then_inc(z_exp, 1)

            def group_rows(c):
                act.wait_ge(sT_mm, c + 1)
                act.wait_ge(soft_out, c * 64)
                act.wait_ge(s_lo, c)
                copy(sTs[0:E + F, :], PS[0:E + F, 2, :]).then_inc(sT_cp, 1)

            def group_rows_high(c):
                act.wait_ge(sT_cp, c + 1)
                copy(sfs[0:E, 0, :], sTs[0:E, :]).then_inc(s_hi, 1)

            def g_high(e, bank=pG):
                act.wait_ge(g_mm, e + 1)
                act.wait_ge(a3_ok, e)
                act.wait_ge(g3g_ok, e)
                act.wait_ge(g3u_ok, e)
                copy(Gh[:, :], bank[:, 0:XW]).then_inc(g_hi, 1)

            def phase1(c, first, last):
                if not first:
                    routed_rows(c - 1)
                shared_silu(c, 0)
                act.wait_ge(tl_mm, c)
                act.wait_ge(rl_zero, 1)
                copy(RLs[0:E // 2, :], PS[ROUTER, 4, :])
                copy(RLs[E // 2:E, :], PS[ROUTER, 5, :]).then_inc(rl_cp, 1)
                if not last:
                    condition_high(c + 1)
                shared_high(c, 0, first)
                shared_silu(c, 1)
                if last:
                    g_high(0, pA)
                act.wait_ge(dl_ok, c + 1)
                act.activation(ex, ex, ACT.Exp).then_inc(ex_ok, 1)
                if not first:
                    groups_exp(c - 1)
                shared_high(c, 1, first)
                if not last:
                    h_high(c + 1)
                shared_silu(c, 2)
                if not first:
                    group_rows(c - 1)
                shared_high(c, 2, first)
                if not first:
                    group_rows_high(c - 1)

            chunks(act, phase1)
            routed_rows(NCH - 1)

            def adapters_high(n):
                g, u = slice(0, KR), slice(KR, P)
                act.wait_ge(ap_ok[n.p], n.now)
                act.wait_ge(gB_mm[n.p], n.same)
                copy(Vg[n.p][g, :], ap[g, :]).then_inc(vg_hi[n.p], 1)
                copy(Vu[n.p][u, :], ap[u, :]).then_inc(vu_hi[n.p], 1)

            def adapters_high_again(n):
                g, u = slice(0, KR), slice(KR, P)
                copy(Xg[n.p][g, :], ap[g, :]).then_inc(xg_hi[n.p], 1)
                copy(Xu[n.p][u, :], ap[u, :]).then_inc(xu_hi[n.p], 1)

            def tail_silu(n):
                act.wait_ge(gC_mm[n.p], n.now)
                act.wait_ge(mulC[1 - n.p], n.last)
                act.activation(sC[TAILS, :], pC[0:TAIL, :], ACT.Silu).then_inc(silC[n.p], 1)

            for prev, cur, nxt, (t, _j), more in steps(act):
                if prev is None:
                    act.wait_ge(sg_mm, 3 * NCH)
                    adapters_high(cur)
                    groups_exp(NCH - 1)
                    adapters_high_again(cur)
                    load_silu()
                    act.wait_ge(zeros_ok, 4)
                    tail_silu(cur)
                    group_rows(NCH - 1)
                    group_rows_high(NCH - 1)
                    adapters_high(nxt)
                else:
                    act.wait_ge(ad_mm[prev.p], prev.now)
                    act.wait_ge(ad_sum[1 - prev.p], prev.last)
                    copy(adc[0:KR, :], pad[KR:P, :]).then_inc(ad_cp[prev.p], 1)
                    with when(act, t, (15, 16), more):
                        adapters_high(nxt)
                    act.wait_ge(adp_ok[prev.p], prev.now)
                    act.wait_ge(y_mm[prev.p], prev.same)
                    copy(Rhi[prev.p][0:KR, :], adp[0:KR, :]).then_inc(ad_hi[prev.p], 1)
                    with when(act, t, (16,), more):
                        tail_silu(cur)
                with when(act, t, (15, 16), more):
                    adapters_high_again(nxt)
                with when(act, t, (16,), more):
                    act.wait_ge(gA_mm[cur.p], cur.now)
                    act.wait_ge(mulA[1 - cur.p], cur.last)
                    act.activation(sA, pA, ACT.Silu).then_inc(silA[cur.p], 1)
                    act.wait_ge(mulC[cur.p], cur.now)
                    act.wait_ge(y_mm[cur.p], cur.same)
                    copy(Rhi[cur.p][TAILS, :], mC[TAILS, :]).then_inc(hiC[cur.p], 1)
                    act.wait_ge(ad_mm[1 - cur.p], cur.last)
                    copy(tail2[0:TAIL, :], mC[TAILS, :]).then_inc(thiC[cur.p], 1)
                    act.wait_ge(mulA[cur.p], cur.now)
                    copy(Ahi[cur.p], mA).then_inc(hiA[cur.p], 1)
                    act.wait_ge(loC[cur.p], cur.now)
                    copy(tail2[TAILS, :], f32(Rlo[cur.p][TAILS, :])).then_inc(tloC[cur.p], 1)
                if prev is None:
                    g_high(1)
                if t in (8, 16):
                    with act.If(more):
                        g_high(cur.e + 1)

        @block.vector
        def _(dve):
            sub = ALU.subtract

            def condition_sums(c):
                xs = y[:, :, bass.ds(c * CH, CH)].rearrange("p k (b s) -> p k b s", s=SEQ)
                dve.wait_ge(x_in, c * 16 + 16)
                dve.wait_ge(xsum_ok, c)
                dve.tensor_reduce(vs.rearrange("p (k b) -> p k b", k=KH), xs, AX, ALU.add).then_inc(vsum_ok, 1)

            def condition_xsum(c):
                xs = y[:, :, bass.ds(c * CH, CH)].rearrange("p k (b s) -> p k b s", s=SEQ)
                dve.wait_ge(vsum_ok, c + 1)
                dve.wait_ge(xc_hi, c)
                dve.wait_ge(xc_lo, c)
                for k in reversed(range(KH)):
                    last = dve.scalar_tensor_tensor(
                        xc[:, k, :].rearrange("p (b s) -> p b s", s=SEQ), xs[:, k], float(SEQ),
                        vs[:, k * CB:(k + 1) * CB].unsqueeze(2).broadcast_to([P, CB, SEQ]), ALU.mult, ALU.add)
                last.then_inc(xsum_ok, 1)

            def condition_q(c, k, ok):
                dve.wait_ge(xsum_ok, c + 1)
                dve.wait_ge(q_ok, 1)
                v = xc[:, k, :].rearrange("p (b s) -> p b s", s=SEQ)
                qc = q[:, k, bass.ds(c * CB, CB)].unsqueeze(2).broadcast_to([P, CB, SEQ])
                dve.tensor_tensor(v, v, qc, ALU.mult).then_inc(ok, 1)

            condition_sums(0)
            condition_xsum(0)
            condition_q(0, 0, xc0_ok)
            dve.wait_ge(xc_hi0, 1)
            dve.tensor_tensor(xcs[:, 1, 0], xc[:, 0], f32(xcs[:, 0, 0]), sub)
            dve.wait_ge(xc_hi, 1)
            dve.tensor_tensor(xcs[:, 1, 1], xc[:, 1], f32(xcs[:, 0, 1]), sub).then_inc(xc_lo, 1)
            dve.wait_ge(consts_in, 16 * 2)
            dve.tensor_copy(invf, invs).then_inc(inv_f, 1)
            dve.wait_ge(inv_f, 1)
            dve.tensor_scalar(invn, invf, 0.0, float(E), ALU.is_lt, ALU.mult).then_inc(inv_n, 1)
            dve.wait_ge(inv_n, 1)
            dve.tensor_tensor(invf, invf, invn, ALU.add).then_inc(inv_w, 1)
            dve.wait_ge(inv_w, 1)
            dve.tensor_scalar(invf, invf, 0.0, float(E - 1), ALU.max, ALU.min).then_inc(inv_c, 1)
            dve.wait_ge(inv_c, 1)
            for n in (0, 1):
                last = dve.tensor_scalar(onehot[:, n * E:(n + 1) * E], invf, rowno[:, n:n + 1], None, ALU.is_equal)
            last.then_inc(onehot_ok, 1)
            dve.wait_ge(h_hi0, 1)
            dve.tensor_tensor(hs[:, 1, 0, 0:CH], hf[:, 0], f32(hs[:, 0, 0, 0:CH]), sub)
            dve.wait_ge(h_hi, 1)
            dve.tensor_tensor(hs[:, 1, 1, 0:CH], hf[:, 1], f32(hs[:, 0, 1, 0:CH]), sub).then_inc(h_lo, 1)

            def shared_mul(c, b):
                n = SB[b][1]
                dve.wait_ge(s_sil, c * 3 + b + 1)
                dve.wait_ge(s_ahi, c * 3 + b)
                dve.wait_ge(s_alo, c * 3 + b)
                dve.tensor_tensor(mS[0:n, :], PS[0:n, 5, :], sS[0:n, :], ALU.mult).then_inc(s_mul, 1)

            def by_group(v):
                return v.rearrange("p j (f k) -> p (j f) k", k=K)

            def groups_masked(c):
                flat = PS[:, 3, TT * E:2 * TT * E].rearrange("p (j e) -> p j e", j=TT)
                dve.wait_ge(fl_mm, c + 1)
                dve.wait_ge(soft_ok, c)
                dve.tensor_scalar(z, flat, 0.0, NEG, ALU.is_equal, ALU.mult).then_inc(z_neg, 1)
                dve.wait_ge(sT_mm, c)
                dve.tensor_reduce(st[:, :, E:E + F], flat.rearrange("p j (f k) -> p j f k", k=K), AX, ALU.add
                                  ).then_inc(tot_ok, 1)
                dve.wait_ge(z_neg, c + 1)
                dve.tensor_tensor(z, z, flat, ALU.add).then_inc(z_all, 1)

            def groups_less_max(c):
                dve.wait_ge(z_all, c + 1)
                dve.tensor_reduce(gm, by_group(z), AX, ALU.max).then_inc(gm_ok, 1)
                dve.wait_ge(gm_ok, c + 1)
                dve.tensor_tensor(by_group(z), by_group(z), gm.unsqueeze(2).broadcast_to([P, TT * F, K]), sub
                                  ).then_inc(z_sub, 1)

            def groups_normalised(c):
                dve.wait_ge(z_exp, c + 1)
                dve.tensor_reduce(gs, by_group(z), AX, ALU.add).then_inc(gs_ok, 1)
                dve.wait_ge(gs_ok, c + 1)
                dve.reciprocal(gs, gs).then_inc(gr_ok, 1)
                dve.wait_ge(gr_ok, c + 1)
                dve.tensor_tensor(st[:, :, 0:E].rearrange("p j (f k) -> p j f k", k=K),
                                  z.rearrange("p j (f k) -> p j f k", k=K),
                                  gs.rearrange("p (j f) -> p j f", j=TT).unsqueeze(3).broadcast_to([P, TT, F, K]),
                                  ALU.mult).then_inc(soft_ok, 1)

            def shared_add(c):
                yc = y[:, :, bass.ds(c * CH, CH)]
                dve.wait_ge(sy_mm, c * 3 + 3)
                dve.tensor_tensor(yc, yc, pY, ALU.add).then_inc(sy_add, 1)

            def g_rows(rows, e, out, cols, ok, bank):
                dve.wait_ge(g_hi, e + 1)
                dve.scalar_tensor_tensor(out[rows, :], f32(Gh[rows, cols]), lomask[rows, :], bank[rows, cols],
                                         ALU.mult, ALU.add).then_inc(ok, 1)

            low, high = slice(0, 3 * K), slice(KR, KR + 3 * K)

            def g_adapters(e, wp, bank=pG):
                g_rows(APK, e, A3[:, wp, :], slice(XA, XA + P), a3_ok, bank)

            def g_gate_up(e, wp, bank=pG):
                dve.wait_ge(piece_lo, e * PIECES + PIECES)
                g_rows(high, e, Wt[wp][:, 1, QGA:QGA + P + CW], slice(XGA, XGA + P + CW), g3g_ok, bank)
                g_rows(low, e, Wt[wp][:, 1, QUB:QUB + P], slice(XUB, XUB + P), g3u_ok, bank)

            def phase1(c, first, last):
                if not last:
                    condition_sums(c + 1)
                if not first:
                    shared_mul(c - 1, 2)
                if not last:
                    condition_xsum(c + 1)
                    condition_q(c + 1, 0, xc0_ok)
                if not first:
                    groups_masked(c - 1)
                shared_mul(c, 0)
                dve.wait_ge(tl_mm, c + 1)
                dve.wait_ge(dl_ok, c)
                dve.wait_ge(rep_ok, c)
                dve.tensor_copy(lg, PS[:, 3, :].rearrange("p (j s) -> p j s", j=TT)[:, :, 0:E]).then_inc(lg_ok, 1)
                dve.wait_ge(lg_ok, c + 1)
                if not first:
                    groups_less_max(c - 1)
                for j in range(TT):
                    mx = dve.max(top[:, j, :], lg[:, j, :])
                mx.then_inc(top_ok, 1)
                dve.wait_ge(top_ok, c + 1)
                dve.memset(top[:, :, TOPK:8], ABSENT).then_inc(absent_ok, 1)
                dve.wait_ge(absent_ok, c + 1)
                dve.wait_ge(ex_ok, c)
                dve.wait_ge(wsel_ok, c)
                dve.tensor_tensor(ex, lg, top[:, :, 0:1].broadcast_to([P, TT, E]), sub).then_inc(dl_ok, 1)
                for j in range(TT):
                    mr = dve.match_replace(rep[:, j, :], top[:, j, :], lg[:, j, :], GONE)
                mr.then_inc(rep_ok, 1)
                shared_mul(c, 1)
                if not first:
                    shared_add(c - 1)
                dve.wait_ge(ex_ok, c + 1)
                dve.tensor_reduce(sm, ex, AX, ALU.add).then_inc(sm_ok, 1)
                dve.wait_ge(sm_ok, c + 1)
                dve.reciprocal(rs, sm).then_inc(rs_ok, 1)
                dve.wait_ge(rep_ok, c + 1)
                dve.wait_ge(wT_mm, c)
                dve.scalar_tensor_tensor(wsel, rep, GONE / 2, ex, ALU.is_le, ALU.mult).then_inc(wsel_ok, 1)
                dve.wait_ge(wsel_ok, c + 1)
                dve.wait_ge(rs_ok, c + 1)
                dve.tensor_tensor(wsel, wsel, rs.unsqueeze(2).broadcast_to([P, TT, E]), ALU.mult).then_inc(wn_ok, 1)
                if not first:
                    groups_normalised(c - 1)
                if last:
                    shared_mul(c, 2)
                    g_adapters(0, 0, pA)
                    g_gate_up(0, 0, pA)

            chunks(dve, phase1)

            def adapters_weighted(n):
                dve.wait_ge(a_mm[n.p], n.now)
                dve.wait_ge(wexp_in[n.p], n.same * 16 + 16)
                dve.wait_ge(vg_hi[1 - n.p], n.last)
                dve.wait_ge(vu_hi[1 - n.p], n.last)
                dve.wait_ge(xg_hi[1 - n.p], n.last)
                dve.wait_ge(xu_hi[1 - n.p], n.last)
                dve.wait_ge(vg_lo[1 - n.p], n.last)
                dve.wait_ge(vu_lo[1 - n.p], n.last)
                dve.tensor_tensor(ap, pa, wexp[n.p], ALU.mult).then_inc(ap_ok[n.p], 1)

            def adapters_low(n):
                g, u = slice(0, KR), slice(KR, P)
                dve.wait_ge(gB_mm[n.p], n.same)
                dve.wait_ge(vg_hi[n.p], n.now)
                dve.tensor_tensor(Vg[n.p][u, :], ap[g, :], f32(Vg[n.p][g, :]), sub).then_inc(vg_lo[n.p], 1)
                dve.wait_ge(vu_hi[n.p], n.now)
                dve.tensor_tensor(Vu[n.p][g, :], ap[u, :], f32(Vu[n.p][u, :]), sub).then_inc(vu_lo[n.p], 1)

            def add_y(n):
                yc = y[:, :, bass.ds(n.c * CH, CH)]
                dve.wait_ge(y_mm[n.p], n.now)
                dve.wait_ge(y_add[1 - n.p], n.last)
                dve.tensor_tensor(yc, yc, pY, ALU.add).then_inc(y_add[n.p], 1)

            for prev, cur, nxt, (t, _j), more in steps(dve):
                if prev is None:
                    dve.wait_ge(wT_mm, NCH)
                    adapters_weighted(cur)
                    groups_masked(NCH - 1)
                    groups_less_max(NCH - 1)
                    dve.wait_ge(sg_mm, 3 * NCH)
                    adapters_low(cur)
                    groups_normalised(NCH - 1)
                    shared_add(NCH - 1)
                with when(dve, t, (15, 16), more):
                    adapters_weighted(nxt)
                if prev is not None:
                    n = prev
                    dve.wait_ge(ad_cp[n.p], n.now)
                    dve.wait_ge(ad_hi[1 - n.p], n.last)
                    dve.wait_ge(ad_lo[1 - n.p], n.last)
                    dve.tensor_tensor(adp[0:KR, :], pad[0:KR, :], adc[0:KR, :], ALU.add).then_inc(ad_sum[n.p], 1)
                    dve.wait_ge(ad_sum[n.p], n.now)
                    dve.wait_ge(wdn_in[n.p], n.same * 16 + 16)
                    dve.tensor_tensor(adp[0:KR, :], adp[0:KR, :], wdn[n.p][0:KR, :], ALU.mult).then_inc(adp_ok[n.p], 1)
                    dve.wait_ge(ad_hi[n.p], n.now)
                    dve.tensor_tensor(Rlo[n.p][0:KR, :], adp[0:KR, :], f32(Rhi[n.p][0:KR, :]), sub
                                      ).then_inc(ad_lo[n.p], 1)
                with when(dve, t, (15, 16), more):
                    adapters_low(nxt)
                if t == 7:
                    g_gate_up(cur.e + 1, 1)
                if t == 15:
                    with dve.If(more):
                        g_gate_up(cur.e + 1, 0)
                if prev is None:
                    dve.wait_ge(zeros_ok, 4)
                with when(dve, t, (16,), more):
                    n = cur
                    dve.wait_ge(scC[n.p], n.now)
                    dve.wait_ge(hiC[1 - n.p], n.last)
                    dve.wait_ge(thiC[1 - n.p], n.last)
                    dve.wait_ge(loC[1 - n.p], n.last)
                    dve.tensor_tensor(mC[TAILS, :], pC[TAILS, :], sC[TAILS, :], ALU.mult).then_inc(mulC[n.p], 1)
                    dve.wait_ge(hiC[n.p], n.now)
                    dve.wait_ge(y_mm[n.p], n.same)
                    dve.tensor_tensor(Rlo[n.p][TAILS, :], mC[TAILS, :], f32(Rhi[n.p][TAILS, :]), sub
                                      ).then_inc(loC[n.p], 1)
                    dve.wait_ge(scA[n.p], n.now)
                    dve.wait_ge(gB_mm[n.p], n.now)
                    dve.wait_ge(hiA[1 - n.p], n.last)
                    dve.wait_ge(loA[1 - n.p], n.last)
                    dve.tensor_tensor(mA, pB, sA, ALU.mult).then_inc(mulA[n.p], 1)
                    dve.wait_ge(hiA[n.p], n.now)
                    dve.tensor_tensor(Alo[n.p], mA, f32(Ahi[n.p]), sub).then_inc(loA[n.p], 1)
                if prev is not None:
                    add_y(prev)
                if prev is None:
                    g_adapters(1, 1)
                    dve.wait_ge(soft_out, 64 * NCH)
                if t in (8, 16):
                    with dve.If(more):
                        g_adapters(cur.e + 1, 1 - cur.w)

        @block.gpsimd
        def _(pool):
            sub = ALU.subtract

            pool.memset(seed[:, 0:1], 0.0).then_inc(seed_ok, 1)
            pool.memset(RLs, 0.0).then_inc(rl_zero, 1)

            def condition_q(c):
                pool.wait_ge(q_ok, 1)
                pool.wait_ge(xsum_ok, c + 1)
                v = xc[:, 1, :].rearrange("p (b s) -> p b s", s=SEQ)
                qc = q[:, 1, bass.ds(c * CB, CB)].unsqueeze(2).broadcast_to([P, CB, SEQ])
                pool.tensor_tensor(v, v, qc, ALU.mult).then_inc(xc_ok, 1)

            def condition_low(c):
                pool.wait_ge(xc_hi, c + 1)
                pool.tensor_tensor(xcs[:, 1], xc, f32(xcs[:, 0]), sub).then_inc(xc_lo, 1)

            def h_low(c):
                pool.wait_ge(h_hi, c + 1)
                cols = bass.ds(c * CH, CH)
                pool.tensor_tensor(hs[:, 1, :, cols], hf, f32(hs[:, 0, :, cols]), sub).then_inc(h_lo, 1)

            def fold(e):
                pool.wait_ge(raw_in, e * 48 + 48)
                pool.tensor_tensor(raw[:, QB:QB + QW], raw[:, QB:QB + QW], scb[:, 0:QW], ALU.mult).then_inc(foldQ, 1)
                r = raw[0:KR, DN + H:DN + 2 * H]
                pool.tensor_tensor(r, r, scb[0:KR, QW:QW + H], ALU.mult).then_inc(foldR, 1)

            def piece(e, wp, z, before):
                cols = bass.ds(z * PW, PW)
                pool.wait_ge(foldQ, e + 1)
                pool.wait_ge(foldR, e + 1)
                if before is not None:
                    pool.wait_ge(y_mm[1], before)
                pool.tensor_copy(Wt[wp][:, 0, cols], raw[:, cols]).then_inc(piece_hi, 1)
                pool.wait_ge(piece_hi, e * PIECES + z + 1)
                pool.tensor_tensor(Wt[wp][:, 1, cols], raw[:, cols], f32(Wt[wp][:, 0, cols]), sub).then_inc(piece_lo, 1)

            def adapter_weights(e, wp):
                src = raw[:, ADR:MU].rearrange("p (k m) -> p k m", k=2)
                pool.tensor_copy(ADt[:, wp, :, 0:KR], src).then_inc(adw_hi, 1)
                pool.wait_ge(adw_hi, e + 1)
                pool.tensor_tensor(ADt[:, wp, :, KR:P], src, f32(ADt[:, wp, :, 0:KR]), sub).then_inc(adw_lo, 1)

            condition_q(0)
            pool.wait_ge(boot_hi, 1)
            pool.tensor_tensor(W2s[:, 1].rearrange("p k m -> p (k m)"), raw[:, BW2:BSG],
                               f32(W2s[:, 0].rearrange("p k m -> p (k m)")), sub).then_inc(w2_lo, 1)
            pool.wait_ge(boot_hi, 2)
            pool.tensor_tensor(SGs[:, 1].rearrange("p k m -> p (k m)"), raw[:, BSG:BSD],
                               f32(SGs[:, 0].rearrange("p k m -> p (k m)")), sub).then_inc(boot_lo, 1)
            pool.wait_ge(boot_hi, 3)
            pool.tensor_tensor(SDs[:, 1].rearrange("p b m -> p (b m)"), SDraw,
                               f32(SDs[:, 0].rearrange("p b m -> p (b m)")), sub).then_inc(boot_lo, 1)

            def shared_low(c, b):
                n = SB[b][1]
                pool.wait_ge(s_ahi, c * 3 + b + 1)
                pool.tensor_tensor(hSs[0:n, b, 1, :], mS[0:n, :], f32(hSs[0:n, b, 0, :]), sub).then_inc(s_alo, 1)

            def group_rows_low(c):
                pool.wait_ge(s_hi, c + 1)
                pool.wait_ge(soft_out, c * 64)
                pool.tensor_tensor(sfs[0:E, 1, :], sTs[0:E, :], f32(sfs[0:E, 0, :]), sub).then_inc(s_lo, 1)

            def phase1(c, first, last):
                if last:
                    adapter_weights(0, 0)
                else:
                    condition_q(c + 1)
                    condition_low(c + 1)
                shared_low(c, 0)
                if not first and not last:
                    piece(0, 0, c - 1, None)
                shared_low(c, 1)
                if not last:
                    h_low(c + 1)
                else:
                    pool.wait_ge(sg_mm, 3 * NCH)
                    for p in (0, 1):
                        pool.memset(f32(Xu[p][0:KR, :]), 0.0).then_inc(zeros_ok, 1)
                shared_low(c, 2)
                if first:
                    fold(0)
                else:
                    group_rows_low(c - 1)

            chunks(pool, phase1)
            pool.memset(f32(tail2[:, :]), 0.0).then_inc(zeros_ok, 1)
            pool.wait_ge(sT_mm, NCH)
            pool.wait_ge(fl_mm, NCH)
            pool.memset(sC, 0.0).then_inc(zeros_ok, 1)
            pool.wait_ge(zeros_ok, 4)
            for prev, cur, nxt, (t, j), more in steps(pool):
                with when(pool, t, (16,), more):
                    pool.wait_ge(scl_in[cur.p], cur.same * 16 + 16)
                    pool.wait_ge(silC[cur.p], cur.now)
                    pool.tensor_tensor(sC, sC, scl[cur.p], ALU.mult).then_inc(scC[cur.p], 1)
                    if prev is None:
                        group_rows_low(NCH - 1)
                    pool.wait_ge(silA[cur.p], cur.now)
                    pool.tensor_tensor(sA, sA, scl[cur.p], ALU.mult).then_inc(scA[cur.p], 1)
                if t == 0:
                    fold(1)
                    pool.wait_ge(soft_out, 64 * NCH)
                if t in (8, 16):
                    with pool.If(more):
                        fold(cur.e + 1)
                if j is not None:
                    with when(pool, t, (9, 10), more):
                        piece(cur.e + 1, 1 - cur.w, j * 2 + (t - 1) % NCH, cur.e * (NCH // 2))
                if t == 7:
                    adapter_weights(cur.e + 1, 1)
                if t == 15:
                    with pool.If(more):
                        adapter_weights(cur.e + 1, 0)


def kernel(x, cond_1024, L0_cond_W3, L0_cond_b3, L0_cond_W2, L0_cond_b2, L0_ffn_gate_weight, L0_ffn_inv_mapping,
           L0_ffn_mask_up_W, L0_ffn_gate_W, L0_ffn_gate_qa, L0_ffn_gate_qb, L0_ffn_gate_scale, L0_ffn_up_W,
           L0_ffn_up_qa, L0_ffn_up_qb, L0_ffn_up_scale, L0_ffn_down_W, L0_ffn_down_qa, L0_ffn_down_qb,
           L0_ffn_down_scale, L0_ffn_sh_gate_W, L0_ffn_sh_up_W, L0_ffn_sh_down_W):
    import numpy as np
    import concourse.bacc as bacc
    from concourse.bass_utils import run_bass_kernel_spmd as run

    f = np.float32

    def tiles(a):
        return a.reshape(-1, P, a.shape[-1]).transpose(1, 0, 2)

    def T(a):
        return np.swapaxes(np.asarray(a), -1, -2)

    def rk(a):
        return np.asarray(a).transpose(0, 3, 1, 2).reshape(F, KR, a.shape[2])

    x = np.asarray(x)
    xT = tiles(T(x.reshape(TOKENS, H)))
    boot = np.zeros((P, BOOT), f)
    boot[:, BW2:BSG] = tiles(np.asarray(L0_cond_W2)).reshape(P, -1)
    sg = boot[:, BSG:BSD].reshape(P, KH, 3, 2, P)
    for g, w in enumerate((L0_ffn_sh_gate_W, L0_ffn_sh_up_W)):
        for b, (at, n) in enumerate(SB):
            sg[:, :, b, g, 0:n] = tiles(T(w))[:, :, at:at + n]
        sg[:, :, 0, g, ROUTER] = tiles(T(L0_ffn_gate_weight))[:, :, g * E // 2:(g + 1) * E // 2]
    boot[:, BSG:BSD] = sg.reshape(P, -1)
    sd = T(L0_ffn_sh_down_W)
    for b, (at, n) in enumerate(SB):
        boot[0:n, BSD + b * H:BSD + (b + 1) * H] = sd[at:at + n]

    raw = np.zeros((F, P, RAWW), f)
    gW, uW = (T(w).reshape(F, KH, P, I) for w in (L0_ffn_gate_W, L0_ffn_up_W))
    qa = [rk(np.swapaxes(np.asarray(w), 2, 3)).transpose(0, 2, 1).reshape(F, KH, P, KR)
          for w in (L0_ffn_gate_qa, L0_ffn_up_qa)]
    mu = np.asarray(L0_ffn_mask_up_W).reshape(F, KH, P, K)
    for k in range(KH):
        o = k * XW
        raw[:, :, o + XA:o + XA + KR] = qa[0][:, k]
        raw[:, :, o + XA + KR:o + XA + P] = qa[1][:, k]
        raw[:, :, o + XGA:o + XGA + P] = gW[:, k, :, 0:P]
        raw[:, :, o + XC:o + XC + TAIL] = gW[:, k, :, P:I]
        raw[:, :, o + XC + KR:o + XC + CW] = uW[:, k, :, P:I]
        raw[:, :, o + XUB:o + XUB + P] = uW[:, k, :, 0:P]
        for row in (0, KR, P - 32):
            for part in range(3):
                at = MU + k * P + row + part * K
                raw[:, :, at:at + K] = mu[:, k]
    gq, uq = (rk(w) for w in (L0_ffn_gate_qb, L0_ffn_up_qb))
    scale = np.zeros((F, QW + H), f)
    gs, us = np.asarray(L0_ffn_gate_scale), np.asarray(L0_ffn_up_scale)
    for half in (0, KR):
        rows = slice(half, half + KR)
        raw[:, rows, QGA:QGA + P] = gq[:, :, 0:P]
        raw[:, rows, QGC:QGC + TAIL] = gq[:, :, P:I]
        raw[:, rows, QUB:QUB + P] = uq[:, :, 0:P]
        raw[:, rows, QUC + KR:QUC + CW] = uq[:, :, P:I]
    scale[:, QGA - QB:QGA - QB + P] = gs[:, 0:P]
    scale[:, QGC - QB:QGC - QB + TAIL] = gs[:, P:I]
    scale[:, QUB - QB:QUB - QB + P] = us[:, 0:P]
    scale[:, QUC - QB + KR:QUC - QB + CW] = us[:, P:I]
    scale[:, QW:] = np.asarray(L0_ffn_down_scale)
    dW = T(L0_ffn_down_W)
    raw[:, :, DN:DN + H] = dW[:, 0:P]
    raw[:, 0:KR, DN + H:DN + 2 * H] = rk(L0_ffn_down_qb)
    raw[:, KR:CW, DN + H:DN + 2 * H] = dW[:, P:I]
    da = rk(np.swapaxes(np.asarray(L0_ffn_down_qa), 2, 3)).transpose(0, 2, 1)
    raw[:, :, ADR:ADR + KR] = da[:, 0:P]
    for row in (0, KR):
        raw[:, row:row + TAIL, ADR + KR:ADR + 2 * KR] = da[:, P:I]

    consts = np.zeros((P, CONSTS), f)
    consts[:, 0:P] = np.eye(P)
    for row in (0, KR, P - 32):
        consts[row + 2 * K:row + 3 * K, P] = -1.0
    consts[:, P + 1] = np.arange(P)
    consts[:, P + 2] = np.arange(P) - E
    vecs = np.concatenate([np.asarray(v).reshape(KH, P).T for v in (L0_cond_b3, L0_cond_b2)], axis=1)

    arrays = {
        "xT": xT, "condT": T(cond_1024), "W3": np.asarray(L0_cond_W3), "vecs": vecs, "consts": consts,
        "inv": np.asarray(L0_ffn_inv_mapping), "boot": boot, "raw": raw.reshape(F * P, RAWW), "scale": scale,
    }
    arrays = {"in_" + n: np.ascontiguousarray(a) for n, a in arrays.items()}
    nc = bacc.Bacc("TRN2", target_bir_lowering=False, num_devices=1)
    args = [nc.dram_tensor(n, a.shape, mybir.dt.from_np(a.dtype), kind="ExternalInput").ap() for n, a in arrays.items()]
    out = nc.dram_tensor("out_T", (P, KH, TOKENS), F32, kind="ExternalOutput").ap()
    build(nc, *args, out)
    got = run(nc, [arrays], core_ids=[0]).results[0]["out_T"]
    return got.transpose(2, 1, 0).reshape(BATCH, SEQ, H)
```
